# Optimizing a Trainium2 kernel written in Bass

```python
import numpy as np
import jax
import jax.numpy as jnp

def _softmax(x, axis=-1):
    return jax.nn.softmax(x, axis=axis)
def _gelu(x):
    return jax.nn.gelu(x, approximate=True)
def _silu(x):
    return jax.nn.silu(x)
def _sigmoid(x):
    return jax.nn.sigmoid(x)
def _layernorm(x, axis=-1, eps=1e-5):
    m = jnp.mean(x, axis=axis, keepdims=True)
    v = jnp.var(x, axis=axis, keepdims=True)
    return (x - m) / jnp.sqrt(v + eps)
def _scatter_add(tgt, idx, src, axis=0):
    return tgt.at[idx].add(src)
def _segment_sum(src, seg, n):
    return jax.ops.segment_sum(src, seg, n)

kernel_name = 'mk_adj_resnorm_d2_adj_128_f85322'

def setup_inputs(seed: int = 0):
    np.random.seed(seed)
    _w = jnp.asarray
    def _rec_inputs():
        import jax
        import jax.numpy as jnp
        _gk = jax.random.key(seed)
        x = -0.000929 + 1 * jax.random.normal(jax.random.fold_in(_gk, 1), (8192, 128), jnp.float32)
        _a = jax.random.bernoulli(jax.random.fold_in(_gk, 2), 0.00195312, (8192, 8192))
        _a = jnp.logical_or(_a, jnp.swapaxes(_a, -1, -2))
        _a = jnp.logical_or(_a, jnp.eye(8192, dtype=bool))
        _af = _a.astype(jnp.float32)
        adj = _af
        return x, adj
    x, adj = _rec_inputs()
    def _L0_gnn_setup():
        import jax, jax.numpy as jnp
        import numpy as np
        N, EMB, HID = (8192, 128, 128)
        key = jax.random.key(seed)
        k1, k2, k3, k4, k5, k6, k7, k8 = jax.random.split(key, 8)
        inlayer = jax.random.normal(k1, (N, EMB), dtype=jnp.float32)
        inlayer2 = jax.random.normal(k2, (N, 2 * EMB), dtype=jnp.float32)
        adj_mat = jax.random.randint(k3, (N, N), 0, 2).astype(jnp.float32)
        W1 = jax.random.normal(k4, (HID, 2 * EMB), dtype=jnp.float32) / np.sqrt(2 * EMB)
        w2 = jax.random.normal(k5, (HID,), dtype=jnp.float32) / np.sqrt(HID)
        b2 = jax.random.normal(k6, (), dtype=jnp.float32) * 0.01
        w3 = jax.random.normal(k7, (HID,), dtype=jnp.float32) / np.sqrt(HID)
        b3 = jax.random.normal(k8, (), dtype=jnp.float32) * 0.01
        return {'inlayer': inlayer, 'inlayer2': inlayer2, 'adj_mat': adj_mat, 'W1': W1, 'w2': w2, 'b2': b2, 'w3': w3, 'b3': b3}
    _L0_gnn_all = _L0_gnn_setup()
    _L0_gnn_in = {k: v for k, v in _L0_gnn_all.items() if k in ('inlayer2', 'W1', 'w2', 'b2', 'w3', 'b3', )}
    del _L0_gnn_all

    def _L1_gnn_setup():
        import jax, jax.numpy as jnp
        import numpy as np
        N = 8192
        D = 128
        EDGE_P = 0.005
        key = jax.random.key(seed)
        kx, ka, kb = jax.random.split(key, 3)
        x = jax.random.normal(kx, (N, D), dtype=jnp.float32)
        adj = (jax.random.uniform(ka, (N, N)) < EDGE_P).astype(jnp.float32)
        adj = jnp.maximum(adj, jnp.eye(N, dtype=jnp.float32))
        beta = jax.random.uniform(kb, (1,), dtype=jnp.float32)
        return {'x': x, 'adj': adj, 'beta': beta}
    _L1_gnn_all = _L1_gnn_setup()
    _L1_gnn_in = {k: v for k, v in _L1_gnn_all.items() if k in ('beta', )}
    del _L1_gnn_all

    return {
        "x": x,
        "adj": adj,
        "L0_gnn_inlayer2": _L0_gnn_in["inlayer2"],
        "L0_gnn_W1": _L0_gnn_in["W1"],
        "L0_gnn_w2": _L0_gnn_in["w2"],
        "L0_gnn_b2": _L0_gnn_in["b2"],
        "L0_gnn_w3": _L0_gnn_in["w3"],
        "L0_gnn_b3": _L0_gnn_in["b3"],
        "L1_gnn_beta": _L1_gnn_in["beta"],
    }

def reference(x, adj, L0_gnn_inlayer2, L0_gnn_W1, L0_gnn_w2, L0_gnn_b2, L0_gnn_w3, L0_gnn_b3, L1_gnn_beta):
    import jax
    import jax.numpy as jnp
    def _L0_gnn_ref(inlayer, inlayer2, adj_mat, W1, w2, b2, w3, b3):
        import jax, jax.numpy as jnp
        import numpy as np
        N, EMB, HID = (8192, 128, 128)
        in_fts = jnp.einsum('ne,he->nh', inlayer2, W1)
        f1 = in_fts @ w2 + b2
        f2 = in_fts @ w3 + b3
        logits = f1[:, None] + f2[None, :]
        logits = adj_mat * logits
        bias_mat = -1000000000.0 * (1.0 - (adj_mat > 0).astype(jnp.float32))
        coefs = jax.nn.softmax(jax.nn.leaky_relu(logits, 0.01) + bias_mat, axis=1)
        vals = coefs @ inlayer
        return vals

    def _L1_gnn_ref(x, adj, beta):
        import jax, jax.numpy as jnp
        import numpy as np
        N = 8192
        D = 128
        EDGE_P = 0.005
        norm2 = jnp.linalg.norm(x, axis=1, keepdims=True)
        cos = beta[0] * (x @ x.T) / (norm2 @ norm2.T + 1e-07)
        masked = cos + (1.0 - adj) * -1000000000.0
        P = jax.nn.softmax(masked, axis=1)
        return P @ x

    x = _layernorm(x + _L0_gnn_ref(x, L0_gnn_inlayer2, adj, L0_gnn_W1, L0_gnn_w2, L0_gnn_b2, L0_gnn_w3, L0_gnn_b3), axis=-1)
    x = _layernorm(x + _L1_gnn_ref(x, adj, L1_gnn_beta), axis=-1)
    return x


_drawn_inputs = setup_inputs


def setup_inputs(seed=0):
    import zlib

    import numpy as np

    out = dict(_drawn_inputs(seed))
    spreads = {}
    factors = {}
    for name, (base, spread) in spreads.items():
        noise = np.random.default_rng([zlib.crc32(name.encode()), seed]).standard_normal(out[name].shape)
        drawn = base * np.exp(spread * noise) if base else spread * noise
        out[name] = jnp.asarray(drawn.astype(out[name].dtype))
    for name, factor in factors.items():
        out[name] = (out[name] * factor).astype(out[name].dtype)
    return out
```

```python
from contextlib import ExitStack

import numpy as np

import concourse.bass as bass
from concourse import mybir

F32 = mybir.dt.float32
BF16 = mybir.dt.bfloat16
F16 = mybir.dt.float16
U16 = mybir.dt.uint16
ALU = mybir.AluOpType
ACT = mybir.ActivationFunctionType
AX_X = mybir.AxisListType.X
ds = bass.ds

P = 128
N = 8192
D = 128
E2 = 256
JT = N // P
BLK = 512
NB = N // BLK
TB = BLK // P
GJ = 2
NG = JT // GJ
GW = GJ * BLK
CJ = 16
NC = JT // CJ
CG = CJ // GJ
BITS = 16
WPT = P // BITS
WB = BLK // BITS
SJ = 4
NS = JT // SJ
XA = D + 1
M0 = 4 * XA
M1 = 264
ONE = 7
HI = 8
LO = HI + D
M1N = M1 - ONE
PC = 8
SLOPE = 0.01
EPS = 1e-5
COS_EPS = 1e-7
BIG = 2.0 ** 100
TINY = 2.0 ** -100
XS = 32.0
MR = 4
E0 = 12
E1 = 7


def wait(eng, sem, value):
    if isinstance(value, int) and value <= 0:
        return
    eng.wait_ge(sem, value)


def build_program(nc, x, adj, in2, w1, w2, b2, w3, b3, beta, ident_d, powers_d, out):
    x_rows = x.rearrange("(t p) d -> p t d", p=P)
    in2_rows = in2.rearrange("(t p) e -> p t e", p=P)
    out_rows = out.rearrange("(t p) d -> p t d", p=P)
    adj_rows = adj.rearrange("(b p t) c -> b p t c", p=P, t=TB)
    f1_dram = nc.dram_tensor("f1_scratch", (JT, P), F32, kind="Internal").ap()
    f1_blocks = f1_dram.rearrange("(b t) p -> b (t p)", t=TB)
    xs_dram = nc.dram_tensor("x1_scratch", (N, 4 * D), F16, kind="Internal").ap()
    xs_rows = xs_dram.rearrange("(t p) d -> p t d", p=P)

    with ExitStack() as whole:
        def keep(name, shape, dtype):
            return whole.enter_context(nc.sbuf_tensor(name, shape, dtype))

        bits = keep("bits", [P, NB * JT * WB], U16)
        ident16 = keep("ident16", [P, P], F16)
        ones16 = keep("ones16", [P, P], BF16)
        mhalf = keep("mhalf", [P, TB], F32)
        beta_scale = keep("beta_scale", [P, 1], F32)
        beta_shift = keep("beta_shift", [P, 1], F32)

        with ExitStack() as first:
            def sb(name, shape, dtype):
                return first.enter_context(nc.sbuf_tensor(name, shape, dtype))

            t = dict(
                mov=sb("mov0", [P, JT, M0], BF16),
                f2big=sb("f2big", [P, JT], F32),
                alpha=sb("alpha", [P, JT], F32),
                gamma=sb("gamma", [P, JT], F32),
                powers=sb("powers", [P, WPT], BF16),
                tiny_hi=sb("tiny_hi0", [1, 2 * XA], BF16),
                tiny_lo=sb("tiny_lo0", [1, 2 * XA], BF16),
            )
            prepare(nc, x_rows, in2_rows, w1, w2, b2, w3, b3, beta, ident_d, powers_d, f1_dram,
                    ident16, ones16, mhalf, beta_scale, beta_shift, t)
            layer0(nc, adj_rows, x_rows, f1_blocks, xs_rows, bits, ones16, mhalf, t)
        layer1(nc, xs_rows, out_rows, bits, ident16, ones16, mhalf, beta_scale, beta_shift)


def prepare(nc, x_rows, in2_rows, w1, w2, b2, w3, b3, beta, ident_d, powers_d, f1_dram,
            ident16, ones16, mhalf, beta_scale, beta_shift, t):
    mov, f2big, alpha, gamma = t["mov"], t["f2big"], t["alpha"], t["gamma"]
    tiny_hi, tiny_lo = t["tiny_hi"], t["tiny_lo"]
    STEPS = JT // PC
    with ExitStack() as ctx:
        def sb(name, shape, dtype):
            return ctx.enter_context(nc.sbuf_tensor(name, shape, dtype))

        def sem(name):
            return ctx.enter_context(nc.semaphore(name))

        ident = sb("ident", [P, P], F32)
        powers32 = sb("powers32", [P, WPT], F32)
        ones32 = sb("ones32", [P, P], F32)
        w1_sb = sb("w1_sb", [P, E2], F32)
        w_col = sb("w_col", [P, 2], F32)
        w_rep = sb("w_rep", [P, 2, P], F32)
        row3 = sb("row3", [1, 3], F32)
        v = sb("v", [P, 2, E2], F32)
        cols3 = sb("cols3", [P, 3], F32)
        in2_ring = sb("in2_ring", [P, 2, PC, E2], F32)
        product = sb("product", [P, 2, E2], F32)
        f_step = sb("f_step", [P, 2, PC], F32)
        f1 = sb("f1", [P, JT], F32)
        f2 = sb("f2", [P, JT], F32)
        small = sb("small", [P, JT], F32)
        row_max = sb("row_max", [P, JT], F32)
        za = sb("za", [P, JT], F32)
        zg = sb("zg", [P, JT], F32)
        mx = sb("mx", [P, 1], F32)
        mx_all = sb("mx_all", [P, 1], F32)
        b_col = sb("b_col", [P, JT], F32)
        d_col = sb("d_col", [P, JT], F32)
        x_ring = sb("x_ring", [P, 2, PC, XA], F32)
        wx = sb("wx", [P, 2, PC, XA], F32)
        f1t = sb("f1t", [JT, P], F32)
        tiny32 = sb("tiny32", [1, 2 * XA], F32)
        ps_v = ctx.enter_context(nc.psum_tensor("ps_v", [P, 2 * E2], F32))
        ps_c = ctx.enter_context(nc.psum_tensor("ps_c", [P, 512], F32))
        ps_f = ctx.enter_context(nc.psum_tensor("ps_f", [P, 512], F32))
        ps_s = ctx.enter_context(nc.psum_tensor("ps_s", [P, 512], F32))

        s_const = sem("s_const")
        s_in2 = [sem("s_in2a"), sem("s_in2b")]
        s_xin = [sem("s_xina"), sem("s_xinb")]
        s_ones = sem("s_ones")
        s_rep = sem("s_rep")
        s_v = sem("s_v")
        s_vsb = sem("s_vsb")
        s_ttr = sem("s_ttr")
        s_f = sem("s_f")
        s_mx = sem("s_mx")
        s_mxall = sem("s_mxall")
        s_chain = sem("s_chain")
        s_exp = sem("s_exp")
        s_f1t = sem("s_f1t")
        s_f1sb = sem("s_f1sb")
        s_f1out = sem("s_f1out")
        s_wx = sem("s_wx")
        s_hi = sem("s_hi")
        s_lo = sem("s_lo")
        s_cs = sem("s_cs")
        s_end = sem("s_end")
        block = ctx.enter_context(nc.Block())

        @block.sync
        def _(sp):
            loads = [(ident[:, :], ident_d), (powers32[:, :], powers_d), (w1_sb[:, :], w1),
                     (w_col[:, 0:1], w2.rearrange("(h o) -> h o", o=1)),
                     (w_col[:, 1:2], w3.rearrange("(h o) -> h o", o=1)),
                     (row3[:, 0:1], b2), (row3[:, 1:2], b3),
                     (row3[:, 2:3], beta.rearrange("(a b) -> a b", a=1))]
            for dst, src in loads:
                sp.dma_start(dst, src).then_inc(s_const, 16)
            with sp.Fori(0, STEPS // 2) as n:
                for s in range(2):
                    k = n * 2 + s
                    sp.wait_ge(s_f, k + 1)
                    sp.dma_start(in2_ring[:, s, :, :], in2_rows[:, ds(k * PC, PC), :]).then_inc(s_in2[s], 16)
            with sp.Fori(0, STEPS // 2) as n:
                for s in range(2):
                    k = n * 2 + s
                    sp.wait_ge(s_cs, k + 1)
                    sp.dma_start(x_ring[:, s, :, 0:D], x_rows[:, ds(k * PC, PC), :]).then_inc(s_xin[s], 16)
            sp.wait_ge(s_f1sb, 1)
            sp.dma_start(f1_dram, f1t[:, :]).then_inc(s_f1out, 16)
            sp.wait_ge(s_f1out, 16)

        @block.tensor
        def _(pe):
            pe.wait_ge(s_ones, 3)
            pe.wait_ge(s_rep, 2)
            pe.wait_ge(s_const, 16 * 8)
            for w in range(2):
                mm = nc.tensor.matmul(ps_v[:, w * E2:(w + 1) * E2], w_rep[:, w, :], w1_sb[:, :], start=True, stop=True)
            mm = nc.tensor.matmul(ps_c[:, 0:3], ones32[0:1, :], row3[:, :], start=True, stop=True)
            mm.then_inc(s_v, 1)
            nc.tensor.matmul(ps_f[:, 0:1], ones32[0:1, :], ones32[0:1, 0:1], start=True, stop=True).then_inc(s_cs, 2)
            pe.wait_ge(s_chain, 5)
            nc.tensor.transpose(ps_f[0:JT, 0:P], f1[:, :], ident[:, :]).then_inc(s_f1t, 1)
            with pe.Fori(0, STEPS // 2) as n:
                for s in range(2):
                    pe.wait_ge(s_xin[s], n * 16 + 16)
                    pe.wait_ge(s_wx, (n * 2 + s) * 2 + 2)
                    for j in range(PC):
                        mm = nc.tensor.matmul(ps_s[0:1, 0:XA], ones32[:, 0:1], x_ring[:, s, j, :],
                                              start=False, stop=False, skip_group_check=True)
                    mm.then_inc(s_cs, 1)

        @block.gpsimd
        def _(pool):
            nc.gpsimd.memset(mhalf[:, :], -0.5)
            pool.wait_ge(s_mx, 1)
            nc.gpsimd.partition_all_reduce(mx_all[:, :], mx[:, :], P, bass.bass_isa.ReduceOp.max).then_inc(s_mxall, 1)

        @block.scalar
        def _(act):
            act.wait_ge(s_v, 1)
            nc.scalar.activation(v[:, :, :], ps_v[:, :].rearrange("p (w e) -> p w e", w=2), ACT.Copy)
            nc.scalar.activation(cols3[:, :], ps_c[:, 0:3], ACT.Copy).then_inc(s_vsb, 1)
            act.wait_ge(s_chain, 1)
            nc.scalar.activation(b_col[:, :], f2[:, :], ACT.Exp)
            nc.scalar.activation(d_col[:, :], f2[:, :], ACT.Exp, scale=SLOPE).then_inc(s_exp, 1)
            act.wait_ge(s_chain, 7)
            nc.scalar.activation(alpha[:, :], za[:, :], ACT.Exp)
            nc.scalar.activation(gamma[:, :], zg[:, :], ACT.Exp).then_inc(s_exp, 1)
            act.wait_ge(s_vsb, 1)
            nc.scalar.activation(beta_scale[:, :], cols3[:, 2:3], ACT.Copy, scale=1.0 / (XS * XS))
            with act.Fori(0, STEPS) as k:
                for w in range(2):
                    act.wait_ge(s_wx, k * 2 + w + 1)
                    nc.scalar.activation(mov[:, ds(k * PC, PC), 2 * w * XA:(2 * w + 1) * XA], wx[:, w, :, :],
                                         ACT.Copy).then_inc(s_hi, 1)

        @block.vector
        def _(dve):
            links = [0]

            def chain(instruction):
                links[0] += 1
                instruction.then_inc(s_chain, 1)
                dve.wait_ge(s_chain, links[0])

            nc.vector.memset(ones16[:, :], 1.0)
            nc.vector.memset(x_ring[:, :, :, D:XA], 1.0)
            nc.vector.memset(ps_s[:, :], 0.0).then_inc(s_ones, 1)
            nc.vector.memset(tiny32[:, :], 0.0).then_inc(s_ones, 1)
            nc.vector.memset(ones32[:, :], 1.0).then_inc(s_ones, 1)
            dve.wait_ge(s_ones, 3)
            nc.vector.memset(small[:, 0:1], 0.0).then_inc(s_f, 2)
            dve.wait_ge(s_const, 16 * 8)
            nc.vector.tensor_copy(ident16[:, :], ident[:, :])
            nc.vector.tensor_copy(t["powers"][:, :], powers32[:, :])
            for w in range(2):
                nc.vector.tensor_scalar(w_rep[:, w, :], ones32[:, :], w_col[:, w:w + 1], None, ALU.mult).then_inc(s_rep, 1)
            dve.wait_ge(s_vsb, 1)
            with dve.Fori(0, STEPS // 2) as n:
                for s in range(2):
                    k = n * 2 + s
                    dve.wait_ge(s_in2[s], n * 16 + 16)
                    for j in range(PC):
                        for w in range(2):
                            c = j * 2 + w
                            if c >= 2:
                                dve.wait_ge(s_ttr, k * 2 * PC + c - 1)
                            elif c == 0:
                                dve.wait_ge(s_f, k + 2)
                            nc.vector.tensor_tensor_reduce(
                                product[:, w, :], in2_ring[:, s, j, :], v[:, w, :], 1.0, 0.0, ALU.mult, ALU.add,
                                f_step[:, w, j:j + 1]).then_inc(s_ttr, 1)
                    dve.wait_ge(s_ttr, (k + 1) * 2 * PC)
                    nc.vector.tensor_copy(f1[:, ds(k * PC, PC)], f_step[:, 0, :])
                    nc.vector.tensor_copy(f2[:, ds(k * PC, PC)], f_step[:, 1, :]).then_inc(s_f, 1)
            dve.wait_ge(s_f, STEPS + 2)
            nc.vector.reduce_max(mx[:, :], f2[:, :], AX_X).then_inc(s_mx, 1)
            dve.wait_ge(s_mxall, 1)
            chain(nc.vector.tensor_scalar(f2[:, :], f2[:, :], mx_all[:, 0:1], None, ALU.subtract))
            chain(nc.vector.tensor_scalar(f1[:, :], f1[:, :], cols3[:, 0:1], cols3[:, 1:2], ALU.add, ALU.add))
            chain(nc.vector.tensor_scalar(f1[:, :], f1[:, :], mx_all[:, 0:1], None, ALU.add))
            chain(nc.vector.tensor_scalar(small[:, :], f1[:, :], SLOPE, None, ALU.mult))
            chain(nc.vector.tensor_tensor(row_max[:, :], f1[:, :], small[:, :], ALU.max))
            chain(nc.vector.tensor_tensor(za[:, :], f1[:, :], row_max[:, :], ALU.subtract))
            chain(nc.vector.tensor_tensor(zg[:, :], small[:, :], row_max[:, :], ALU.subtract))
            chain(nc.vector.tensor_scalar(f2big[:, :], f2[:, :], BIG, None, ALU.mult))
            chain(nc.vector.tensor_scalar(beta_shift[:, :], cols3[:, 2:3], -1.0, None, ALU.mult))
            chain(nc.vector.tensor_tensor(beta_shift[:, :], beta_shift[:, :], cols3[:, 2:3], ALU.min))
            dve.wait_ge(s_f1t, 1)
            nc.vector.tensor_copy(f1t[:, :], ps_f[0:JT, 0:P]).then_inc(s_f1sb, 1)
            dve.wait_ge(s_exp, 1)
            with dve.Fori(0, STEPS // 2) as n:
                for s in range(2):
                    k = n * 2 + s
                    dve.wait_ge(s_xin[s], n * 16 + 16)
                    for w, factor in enumerate((b_col, d_col)):
                        nc.vector.tensor_tensor(
                            wx[:, w, :, :], x_ring[:, s, :, :],
                            factor[:, ds(k * PC, PC)].unsqueeze(2).to_broadcast([P, PC, XA]), ALU.mult).then_inc(s_wx, 1)
                    for w in range(2):
                        dve.wait_ge(s_hi, k * 2 + w + 1)
                        nc.vector.tensor_tensor(
                            mov[:, ds(k * PC, PC), (2 * w + 1) * XA:(2 * w + 2) * XA], wx[:, w, :, :],
                            mov[:, ds(k * PC, PC), 2 * w * XA:(2 * w + 1) * XA], ALU.subtract).then_inc(s_lo, 1)
                    dve.wait_ge(s_lo, k * 2 + 2)
            dve.wait_ge(s_cs, STEPS + 2)
            chain(nc.vector.tensor_scalar(tiny32[:, XA:2 * XA], ps_s[0:1, 0:XA], TINY, None, ALU.mult))
            chain(nc.vector.tensor_copy(tiny_hi[:, :], tiny32[:, :]))
            nc.vector.tensor_tensor(tiny_lo[:, :], tiny32[:, :], tiny_hi[:, :], ALU.subtract).then_inc(s_end, 1)


def norm_rows(nc, dve, s_step, done, rows, stats, mv, ve):
    def statistics():
        dve.wait_ge(s_step, done)
        for i in range(TB):
            ins = nc.vector.bn_stats(stats[:, i, :], rows[:, i, :])
        ins.then_inc(s_step, 1)

    def moments():
        dve.wait_ge(s_step, done + 1)
        nc.vector.memset(ve[:, :], 0.0)
        for i in range(TB):
            ins = nc.vector.bn_aggr(mv[:, i, :], stats[:, i, :])
        ins.then_inc(s_step, 1)

    def variance():
        dve.wait_ge(s_step, done + 2)
        nc.vector.tensor_scalar(ve[:, :], mv[:, :, 1], EPS, None, ALU.add).then_inc(s_step, 1)

    return statistics, moments, variance


def spread_bits(nc, bits, mask, b, c):
    source = bits[:, ds((b * NC + c) * CJ * WB, CJ * WB)].rearrange("p (j w) -> p j w", w=WB)
    target = mask[:, :].rearrange("p (j k w) -> p j k w", k=BITS, w=WB)
    for k in range(BITS):
        shift, op = (14 - k, ALU.logical_shift_left) if k < 15 else (1, ALU.logical_shift_right)
        ins = nc.vector.tensor_scalar(target[:, :, k, :], source, shift, 0x4000, op, ALU.bitwise_and)
    return ins


def layer0(nc, adj_rows, x_rows, f1_blocks, xs_rows, bits, ones16, mhalf, t):
    mov, f2big, alpha, gamma, powers = t["mov"], t["f2big"], t["alpha"], t["gamma"], t["powers"]
    tiny_hi, tiny_lo = t["tiny_hi"], t["tiny_lo"]
    with ExitStack() as ctx:
        def sb(name, shape, dtype):
            return ctx.enter_context(nc.sbuf_tensor(name, shape, dtype))

        def sem(name):
            return ctx.enter_context(nc.semaphore(name))

        stage = sb("stage", [P, 2 * TB * SJ * P], F32)
        mask = sb("mask0", [P, CJ * BLK], U16)
        side = sb("side", [P, 2, GW], BF16)
        upper = sb("upper", [P, MR, GJ, BLK], BF16)
        lower = sb("lower", [P, MR, GJ, BLK], BF16)
        f1_row = sb("f1_row", [P, BLK], F32)
        x_blk = sb("x_blk", [P, TB, D], F32)
        part = sb("part0", [P, TB, XA], F32)
        sums = sb("sums0", [P, TB, XA], F32)
        y = sb("y0", [P, TB, D], F32)
        x1 = sb("x1", [P, TB, D], F32)
        x1_out = sb("x1_out", [P, TB, 4 * D], F16)
        inv = sb("inv0", [P, TB], F32)
        stats = sb("stats0", [P, TB, 6], F32)
        mv = sb("mv0", [P, TB, 2], F32)
        ve = sb("ve0", [P, TB], F32)
        rstd = sb("rstd0", [P, TB], F32)
        n2 = sb("n2", [P, TB], F32)
        rnorm = sb("rnorm", [P, TB], F32)
        acc = ctx.enter_context(nc.psum_tensor("acc0", [P, TB, 512], F32))
        words = ctx.enter_context(nc.psum_tensor("words", [P, 2, 512], F32))
        stage16 = stage[:, :].bitcast(BF16)
        mask16 = mask[:, :].bitcast(BF16)

        s_adj = [sem("s_adj_a"), sem("s_adj_b")]
        s_read = sem("s_read")
        s_bits = sem("s_bits")
        s_f1row = sem("s_f1row")
        s_side = sem("s_side")
        s_mask = sem("s_mask")
        s_upper = sem("s_upper")
        s_lower = sem("s_lower")
        s_used = sem("s_used")
        s_part = sem("s_part")
        s_open = sem("s_open0")
        s_step = sem("s_step0")
        s_x = sem("s_x")
        s_pow = sem("s_pow0")
        s_rn = sem("s_rn")
        s_hi = sem("s_hi0")
        s_st = sem("s_st")
        block = ctx.enter_context(nc.Block())

        @block.sync
        def _(sp):
            def load_adj(b, c):
                s = c % 2
                wait(sp, s_read, b * NS + (c - 1))
                sp.dma_start(stage[:, s * TB * SJ * P:(s + 1) * TB * SJ * P].rearrange("p (t c) -> p t c", t=TB),
                             adj_rows[b, :, :, c * SJ * P:(c + 1) * SJ * P]).then_inc(s_adj[s], 16)

            def load_f1(b):
                wait(sp, s_side, b * NG)
                sp.dma_start(f1_row[:, :], f1_blocks[ds(b, 1), :].broadcast_to([P, BLK])).then_inc(s_f1row, 16)

            def load_x(b):
                wait(sp, s_step, (b - 1) * E0 + 2)
                sp.dma_start(x_blk[:, :, :], x_rows[:, ds(b * TB, TB), :]).then_inc(s_x, 16)

            def store_x1(b):
                sp.wait_ge(s_step, (b + 1) * E0)
                sp.dma_start(xs_rows[:, ds(b * TB, TB), :], x1_out[:, :, :]).then_inc(s_st, 16)

            for c in range(NS):
                load_adj(0, c)
            load_f1(0)
            for c in range(NS // 2):
                load_adj(1, c)
            load_x(0)
            for c in range(NS // 2, NS):
                load_adj(1, c)
            with sp.Fori(1, NB - 1) as b:
                load_f1(b)
                for c in range(NS):
                    load_adj(b + 1, c)
                    if c == NS - 3:
                        store_x1(b - 1)
                        load_x(b)
            load_f1(NB - 1)
            store_x1(NB - 2)
            load_x(NB - 1)
            store_x1(NB - 1)
            sp.wait_ge(s_st, 16 * (NB + 1))

        @block.tensor
        def _(pe):
            def pack_load(b, c2, q):
                s, chunk = q % 2, q // (NS // NC)
                pe.wait_ge(s_adj[s], (b * (NS // 2) + c2 * (NS // 4) + q // 2 + 1) * 16)
                if q % (NS // NC) == 0:
                    wait(pe, s_bits, b * NC + c2 * 2 + chunk - 1)
                for j in range(SJ):
                    for i in range(TB):
                        at = 2 * (((s * TB + i) * SJ + j) * P)
                        col = ((q % (NS // NC)) * SJ + j) * WB + i * WPT
                        mm = nc.tensor.matmul(words[:, chunk, col:col + WPT], stage16[:, at + 1:at + 2 * P:2],
                                              powers[:, :], start=True, stop=True, skip_group_check=True)
                mm.then_inc(s_read, 1)

            def block_sums(b, packs):
                pe.wait_ge(s_open, b + 1)
                for i in range(TB):
                    for n, row in enumerate((tiny_hi, tiny_lo)):
                        nc.tensor.matmul(acc[:, i, 0:2 * XA], ones16[0:1, :], row[:, :],
                                         start=(n == 0), stop=False, skip_group_check=True)
                with pe.Fori(0, 2) as c2:
                    for g in range(NG // 2):
                        if packs and g % 2 == 0:
                            pack_load(b + 1, c2, g // 2)
                        pe.wait_ge(s_lower, b * NG + c2 * (NG // 2) + g + 1)
                        for j in range(GJ):
                            for i in range(TB):
                                for w, weights in enumerate((upper, lower)):
                                    for half in range(2):
                                        at = (2 * w + half) * XA
                                        mm = nc.tensor.matmul(
                                            acc[:, i, w * XA:(w + 1) * XA],
                                            weights[:, g % MR, j, i * P:(i + 1) * P],
                                            mov[:, c2 * (JT // 2) + g * GJ + j, at:at + XA],
                                            start=False, stop=False, skip_group_check=True)
                        mm.then_inc(s_used, 1)

            for c2 in range(2):
                for q in range(NS // 2):
                    pack_load(0, c2, q)
            with pe.Fori(0, NB - 1) as b:
                block_sums(b, True)
            block_sums(NB - 1, False)

        @block.scalar
        def _(act):
            def take_words(b, c):
                act.wait_ge(s_read, (b * NC + c + 1) * (NS // NC))
                nc.scalar.activation(
                    bits[:, ds((b * NC + c) * CJ * WB, CJ * WB)].rearrange("p (j g t) -> p j g t", t=TB, g=WPT),
                    words[:, c % 2, :].rearrange("p (j t g) -> p j g t", t=TB, g=WPT), ACT.Copy).then_inc(s_bits, 1)

            def finish_part(b):
                act.wait_ge(s_used, (b + 1) * NG)
                act.wait_ge(s_open, b + 1)
                for i in range(TB):
                    nc.scalar.activation(part[:, i, :], acc[:, i, XA:2 * XA], ACT.Copy,
                                         scale=gamma[:, ds(b * TB + i, 1)]).then_inc(s_part, 1)

            def finish_x1_high(b):
                act.wait_ge(s_step, b * E0 + 6)
                act.wait_ge(s_st, b * 16 + 16)
                nc.scalar.activation(x1_out[:, :, 0:D], x1[:, :, :], ACT.Copy).then_inc(s_hi, 1)

            def finish_xn_high(b):
                act.wait_ge(s_step, b * E0 + 10)
                nc.scalar.activation(x1_out[:, :, 2 * D:3 * D], y[:, :, :], ACT.Copy).then_inc(s_hi, 1)

            def block_sides(b, finish, packs):
                act.wait_ge(s_f1row, (b + 1) * 16)
                for g in range(NG):
                    wait(act, s_upper, b * NG + g - 1)
                    for j in range(GJ):
                        jt = g * GJ + j
                        ins = nc.scalar.activation(side[:, g % 2, j * BLK:(j + 1) * BLK], f1_row[:, :], ACT.Relu,
                                                   bias=f2big[:, jt:jt + 1], scale=BIG)
                    ins.then_inc(s_side, 1)
                    if packs and g % CG == CG - 1:
                        take_words(b + 1, g // CG)
                    if finish:
                        if g == 3:
                            finish_part(b - 1)
                        if g == 11:
                            finish_x1_high(b - 1)
                        if g == 15:
                            finish_xn_high(b - 1)

            for c in range(NC):
                take_words(0, c)
            block_sides(0, False, True)
            with act.Fori(1, NB - 1) as b:
                block_sides(b, True, True)
            block_sides(NB - 1, True, False)
            finish_part(NB - 1)
            finish_x1_high(NB - 1)
            finish_xn_high(NB - 1)

        @block.gpsimd
        def _(pool):
            with pool.Fori(0, NB) as b:
                pool.wait_ge(s_step, b * E0 + 5)
                nc.gpsimd.tensor_tensor(rstd[:, :], ve[:, :], mhalf[:, :], ALU.pow).then_inc(s_pow, 1)
                pool.wait_ge(s_step, b * E0 + 9)
                nc.gpsimd.tensor_tensor(rnorm[:, :], n2[:, :], mhalf[:, :], ALU.pow).then_inc(s_rn, 1)

        @block.vector
        def _(dve):
            def spread(b, c):
                wait(dve, s_lower, b * NG + c * CG)
                dve.wait_ge(s_bits, b * NC + c + 1)
                spread_bits(nc, bits, mask, b, c).then_inc(s_mask, 1)

            def make_upper(b, g):
                m = (g % CG) * GW
                dve.wait_ge(s_side, b * NG + g + 1)
                if g % CG == 0:
                    dve.wait_ge(s_mask, b * NC + g // CG + 1)
                wait(dve, s_used, b * NG + g + 1 - MR)
                nc.vector.tensor_tensor(upper[:, g % MR, :, :].rearrange("p j i -> p (j i)"), side[:, g % 2, :],
                                        mask16[:, m:m + GW], ALU.min).then_inc(s_upper, 1)

            def make_lower(b, g):
                m = (g % CG) * GW
                dve.wait_ge(s_upper, b * NG + g + 1)
                nc.vector.tensor_tensor(lower[:, g % MR, :, :].rearrange("p j i -> p (j i)"), mask16[:, m:m + GW],
                                        upper[:, g % MR, :, :].rearrange("p j i -> p (j i)"),
                                        ALU.subtract).then_inc(s_lower, 1)

            def finish(b):
                base = b * E0

                def gather_sums():
                    dve.wait_ge(s_part, (b + 1) * TB)
                    dve.wait_ge(s_used, (b + 1) * NG)
                    for i in range(TB):
                        ins = nc.vector.scalar_tensor_tensor(
                            out=sums[:, i, :], in0=acc[:, i, 0:XA], scalar=alpha[:, ds(b * TB + i, 1)],
                            in1=part[:, i, :], op0=ALU.mult, op1=ALU.add)
                    ins.then_inc(s_open, 1)

                def invert():
                    dve.wait_ge(s_open, b + 2)
                    nc.vector.reciprocal(inv[:, :], sums[:, :, D]).then_inc(s_step, 1)

                def residual():
                    dve.wait_ge(s_step, base + 1)
                    dve.wait_ge(s_x, (b + 1) * 16)
                    for i in range(TB):
                        ins = nc.vector.scalar_tensor_tensor(
                            out=y[:, i, :], in0=sums[:, i, 0:D], scalar=inv[:, i:i + 1], in1=x_blk[:, i, :],
                            op0=ALU.mult, op1=ALU.add)
                    ins.then_inc(s_step, 1)

                statistics, moments, variance = norm_rows(nc, dve, s_step, base + 2, y, stats, mv, ve)

                def scale_rows():
                    dve.wait_ge(s_pow, b + 1)
                    for i in range(TB):
                        ins = nc.vector.tensor_scalar(x1[:, i, :], y[:, i, :], mv[:, i, 0:1], rstd[:, i:i + 1],
                                                      ALU.subtract, ALU.mult)
                    ins.then_inc(s_step, 1)

                def norm_a():
                    nc.vector.tensor_tensor(n2[:, :], rstd[:, :], rstd[:, :], ALU.mult).then_inc(s_step, 1)

                def norm_b():
                    dve.wait_ge(s_step, base + 7)
                    nc.vector.tensor_tensor(n2[:, :], n2[:, :], mv[:, :, 1], ALU.mult).then_inc(s_step, 1)

                def norm_c():
                    dve.wait_ge(s_step, base + 8)
                    nc.vector.tensor_scalar(n2[:, :], n2[:, :], float(D), COS_EPS, ALU.mult, ALU.add)\
                        .then_inc(s_step, 1)

                def normed_rows():
                    dve.wait_ge(s_rn, b + 1)
                    for i in range(TB):
                        ins = nc.vector.tensor_scalar(y[:, i, :], x1[:, i, :], rnorm[:, i:i + 1], XS,
                                                      ALU.mult, ALU.mult)
                    ins.then_inc(s_step, 1)

                def x1_low():
                    dve.wait_ge(s_hi, b * 2 + 1)
                    nc.vector.tensor_tensor(x1_out[:, :, D:2 * D], x1[:, :, :], x1_out[:, :, 0:D],
                                            ALU.subtract).then_inc(s_step, 1)

                def xn_low():
                    dve.wait_ge(s_hi, b * 2 + 2)
                    nc.vector.tensor_tensor(x1_out[:, :, 3 * D:4 * D], y[:, :, :], x1_out[:, :, 2 * D:3 * D],
                                            ALU.subtract).then_inc(s_step, 1)

                return {1: gather_sums, 2: invert, 3: residual, 4: statistics, 5: moments, 6: variance,
                        8: scale_rows, 9: norm_a, 10: norm_b, 11: norm_c, 13: normed_rows, 14: x1_low, 18: xn_low}

            def block_masks(b, steps):
                for g in range(NG):
                    if g % CG == 0:
                        spread(b, g // CG)
                    make_upper(b, g)
                    if g % CG:
                        make_lower(b, g - 1)
                    if g % CG == CG - 1:
                        make_lower(b, g)
                    if g in steps:
                        steps[g]()

            nc.vector.memset(inv[:, :], 0.0).then_inc(s_open, 1)
            nc.vector.memset(n2[:, :], 0.0).then_inc(s_st, 16)
            block_masks(0, {})
            with dve.Fori(1, NB) as b:
                block_masks(b, finish(b - 1))
            for step in finish(NB - 1).values():
                step()


def layer1(nc, xs_rows, out_rows, bits, ident16, ones16, mhalf, beta_scale, beta_shift):
    TT = 4
    with ExitStack() as ctx:
        def sb(name, shape, dtype):
            return ctx.enter_context(nc.sbuf_tensor(name, shape, dtype))

        def sem(name):
            return ctx.enter_context(nc.semaphore(name))

        mov = sb("mov1", [P, JT, M1], F16)
        xnt = sb("xnt", [P, 2, N], F16)
        xn_in = sb("xn_in", [P, 2, TT, 2 * D], F16)
        mask = sb("mask1", [P, CJ * BLK], U16)
        exps = sb("exps", [P, 2, GW], F32)
        wts = sb("wts", [P, MR * GW], F32)
        low = sb("low", [P, MR, GJ, BLK], BF16)
        tiny32 = sb("tiny32b", [1, M1N], F32)
        tiny_hi = sb("tiny_hi1", [1, M1N], BF16)
        tiny_lo = sb("tiny_lo1", [1, M1N], BF16)
        part = sb("part1", [P, TB, D], F32)
        sums = sb("sums1", [P, TB, D], F32)
        total = sb("total", [P, TB], F32)
        inv = sb("inv1", [P, TB], F32)
        y = sb("y1", [P, TB, D], F32)
        result = sb("result", [P, TB, D], F32)
        stats = sb("stats1", [P, TB, 6], F32)
        mv = sb("mv1", [P, TB, 2], F32)
        ve = sb("ve1", [P, TB], F32)
        rstd = sb("rstd1", [P, TB], F32)
        acc = ctx.enter_context(nc.psum_tensor("acc1", [P, TB, 512], F32))
        scores = ctx.enter_context(nc.psum_tensor("scores", [P, 2, GJ, BLK], F32))
        mask16 = mask[:, :].bitcast(BF16)
        wts_hi = wts[:, :].bitcast(BF16)

        s_mov = sem("s_mov")
        s_one = sem("s_one")
        s_xn = [sem("s_xn_a"), sem("s_xn_b")]
        s_turn = sem("s_turn")
        s_thi = sem("s_thi")
        s_tlo = sem("s_tlo")
        s_cs = sem("s_cs1")
        s_tiny = sem("s_tiny")
        s_scores = sem("s_scores")
        s_exps = sem("s_exps")
        s_mask = sem("s_mask1")
        s_wts = sem("s_wts")
        s_low = sem("s_low")
        s_used = sem("s_used1")
        s_part = sem("s_part1")
        s_open = sem("s_open1")
        s_step = sem("s_step1")
        s_pow = sem("s_pow1")
        s_st = sem("s_st1")
        block = ctx.enter_context(nc.Block())

        @block.sync
        def _(sp):
            for k in range(2):
                sp.dma_start(xn_in[:, k, :, :], xs_rows[:, k * TT:(k + 1) * TT, 2 * D:4 * D]).then_inc(s_xn[k], 16)
            for k in range(2, JT // TT):
                sp.wait_ge(s_turn, k - 1)
                sp.dma_start(xn_in[:, k % 2, :, :], xs_rows[:, k * TT:(k + 1) * TT, 2 * D:4 * D]).then_inc(s_xn[k % 2], 16)

            def store(b):
                sp.wait_ge(s_step, (b + 1) * E1)
                sp.dma_start(out_rows[:, ds(b * TB, TB), :], result[:, :, :]).then_inc(s_st, 16)

            with sp.Fori(0, NB) as b:
                store(b)
            sp.wait_ge(s_st, 16 * (NB + 1))

        @block.tensor
        def _(pe):
            for k in range(JT // TT):
                pe.wait_ge(s_xn[k % 2], (k // 2 + 1) * 16)
                wait(pe, s_thi, k - 1)
                wait(pe, s_tlo, k - 1)
                for half in range(2):
                    for i in range(TT):
                        mm = nc.tensor.matmul(scores[:, k % 2, half, i * P:(i + 1) * P],
                                              xn_in[:, k % 2, i, half * D:(half + 1) * D], ident16[:, :],
                                              start=True, stop=True, skip_group_check=True)
                mm.then_inc(s_turn, 1)
            pe.wait_ge(s_mov, 16 * (JT // PC))
            pe.wait_ge(s_one, 1)
            for j in range(JT):
                mm = nc.tensor.matmul(acc[0:1, 0, 0:M1N], ones16[:, 0:1], mov[:, j, ONE:M1],
                                      start=(j == 0), stop=(j == JT - 1))
            mm.then_inc(s_cs, 1)
            pe.wait_ge(s_thi, JT // TT)
            pe.wait_ge(s_tlo, JT // TT)

            def make_scores(b, g, slot, n):
                wait(pe, s_exps, n - 1)
                for j in range(GJ):
                    for m, (left, right) in enumerate(((0, 0), (0, 1), (1, 0))):
                        mm = nc.tensor.matmul(scores[:, slot, j, :],
                                              xnt[:, left, ds((g * GJ + j) * P, P)],
                                              xnt[:, right, ds(b * BLK, BLK)],
                                              start=(m == 0), stop=(m == 2))
                mm.then_inc(s_scores, 1)

            def weigh(b, g, q):
                pe.wait_ge(s_low, b * NG + g + 1)
                for j in range(GJ):
                    for i in range(TB):
                        at = 2 * (((q % MR) * GJ + j) * BLK + i * P)
                        nc.tensor.matmul(acc[:, i, 0:M1N], wts_hi[:, at + 1:at + 2 * P:2],
                                         mov[:, g * GJ + j, ONE:M1], start=False, stop=False, skip_group_check=True)
                        mm = nc.tensor.matmul(acc[:, i, 0:XA], low[:, q % MR, j, i * P:(i + 1) * P],
                                              mov[:, g * GJ + j, ONE:LO], start=False, stop=False, skip_group_check=True)
                mm.then_inc(s_used, 1)

            def block_sums(b, last):
                def chunk(c, end):
                    for q in range(CG):
                        g = c * CG + q
                        if not end or q < CG - 2:
                            make_scores(b, g + 2, q % 2, b * NG + g + 2)
                        elif not last:
                            make_scores(b + 1, q - (CG - 2), q % 2, b * NG + g + 2)
                        weigh(b, g, q)

                pe.wait_ge(s_open, b + 1)
                for i in range(TB):
                    for n, row in enumerate((tiny_hi, tiny_lo)):
                        nc.tensor.matmul(acc[:, i, 0:M1N], ones16[0:1, :], row[:, :],
                                         start=(n == 0), stop=False, skip_group_check=True)
                with pe.Fori(0, NC - 1) as c:
                    chunk(c, False)
                chunk(NC - 1, True)

            for g in range(2):
                make_scores(0, g, g, g)
            pe.wait_ge(s_tiny, 1)
            with pe.Fori(0, NB - 1) as b:
                block_sums(b, False)
            block_sums(NB - 1, True)

        @block.scalar
        def _(act):
            for k in range(JT // PC):
                act.dma_start(mov[:, k * PC:(k + 1) * PC, HI:M1],
                              xs_rows[:, k * PC:(k + 1) * PC, 0:2 * D]).then_inc(s_mov, 16)
            for k in range(JT // TT):
                act.wait_ge(s_turn, k + 1)
                nc.scalar.activation(xnt[:, 0, k * TT * P:(k + 1) * TT * P], scores[:, k % 2, 0, :],
                                     ACT.Copy).then_inc(s_thi, 1)

            def make_exps(b, g):
                act.wait_ge(s_scores, b * NG + g + 1)
                wait(act, s_wts, b * NG + g - 1)
                nc.scalar.activation(exps[:, g % 2, :], scores[:, g % 2, :, :].rearrange("p j i -> p (j i)"), ACT.Exp,
                                     bias=beta_shift[:, 0:1], scale=beta_scale[:, 0:1]).then_inc(s_exps, 1)

            def finish_part(b):
                act.wait_ge(s_used, (b + 1) * NG)
                act.wait_ge(s_open, b + 1)
                for i in range(TB):
                    nc.scalar.activation(part[:, i, :], acc[:, i, XA:M1N], ACT.Copy).then_inc(s_part, 1)

            def block_exps(b, finish):
                for g in range(NG):
                    make_exps(b, g)
                    if finish and g == 1:
                        finish_part(b - 1)

            block_exps(0, False)
            with act.Fori(1, NB) as b:
                block_exps(b, True)
            finish_part(NB - 1)

        @block.gpsimd
        def _(pool):
            with pool.Fori(0, NB) as b:
                pool.wait_ge(s_step, b * E1 + 6)
                nc.gpsimd.tensor_tensor(rstd[:, :], ve[:, :], mhalf[:, :], ALU.pow).then_inc(s_pow, 1)

        @block.vector
        def _(dve):
            nc.vector.memset(mov[:, :, ONE:HI], 1.0).then_inc(s_one, 1)
            nc.vector.memset(inv[:, :], 0.0).then_inc(s_open, 1)
            nc.vector.memset(total[:, :], 0.0).then_inc(s_st, 16)
            for k in range(JT // TT):
                dve.wait_ge(s_turn, k + 1)
                nc.vector.tensor_copy(xnt[:, 1, k * TT * P:(k + 1) * TT * P], scores[:, k % 2, 1, :]).then_inc(s_tlo, 1)
            dve.wait_ge(s_cs, 1)
            nc.vector.tensor_scalar(tiny32[:, :], acc[0:1, 0, 0:M1N], TINY, None, ALU.mult).then_inc(s_cs, 1)
            dve.wait_ge(s_cs, 2)
            nc.vector.tensor_copy(tiny_hi[:, :], tiny32[:, :]).then_inc(s_cs, 1)
            dve.wait_ge(s_cs, 3)
            nc.vector.tensor_tensor(tiny_lo[:, :], tiny32[:, :], tiny_hi[:, :], ALU.subtract).then_inc(s_tiny, 1)

            def spread(b, c):
                wait(dve, s_wts, b * NG + c * CG)
                spread_bits(nc, bits, mask, b, c).then_inc(s_mask, 1)

            def make_weights(b, g):
                m = (g % CG) * GW
                at = (g % MR) * GW
                dve.wait_ge(s_exps, b * NG + g + 1)
                if g % CG == 0:
                    dve.wait_ge(s_mask, b * NC + g // CG + 1)
                wait(dve, s_used, b * NG + g + 1 - MR)
                nc.vector.tensor_tensor(wts[:, at:at + GW], exps[:, g % 2, :], mask16[:, m:m + GW],
                                        ALU.mult).then_inc(s_wts, 1)

            def make_low(b, g):
                at = (g % MR) * GW
                dve.wait_ge(s_wts, b * NG + g + 1)
                nc.vector.tensor_tensor(low[:, g % MR, :, :].rearrange("p j i -> p (j i)"), wts[:, at:at + GW],
                                        wts_hi[:, 2 * at + 1:2 * (at + GW):2], ALU.subtract).then_inc(s_low, 1)

            def finish(b):
                base = b * E1

                def gather_sums():
                    dve.wait_ge(s_part, (b + 1) * TB)
                    dve.wait_ge(s_used, (b + 1) * NG)
                    nc.vector.tensor_copy(total[:, :], acc[:, :, 0])
                    for i in range(TB):
                        ins = nc.vector.tensor_tensor(sums[:, i, :], acc[:, i, 1:XA], part[:, i, :], ALU.add)
                    ins.then_inc(s_open, 1)

                def invert():
                    dve.wait_ge(s_open, b + 2)
                    nc.vector.reciprocal(inv[:, :], total[:, :]).then_inc(s_step, 1)

                def residual_high():
                    dve.wait_ge(s_step, base + 1)
                    for i in range(TB):
                        ins = nc.vector.scalar_tensor_tensor(
                            out=y[:, i, :], in0=sums[:, i, :], scalar=inv[:, i:i + 1],
                            in1=mov[:, b * TB + i, HI:LO], op0=ALU.mult, op1=ALU.add)
                    ins.then_inc(s_step, 1)

                def residual_low():
                    dve.wait_ge(s_step, base + 2)
                    nc.vector.tensor_tensor(y[:, :, :], y[:, :, :], mov[:, ds(b * TB, TB), LO:M1],
                                            ALU.add).then_inc(s_step, 1)

                statistics, moments, variance = norm_rows(nc, dve, s_step, base + 3, y, stats, mv, ve)

                def scale_rows():
                    dve.wait_ge(s_pow, b + 1)
                    dve.wait_ge(s_st, b * 16 + 16)
                    for i in range(TB):
                        ins = nc.vector.tensor_scalar(result[:, i, :], y[:, i, :], mv[:, i, 0:1], rstd[:, i:i + 1],
                                                      ALU.subtract, ALU.mult)
                    ins.then_inc(s_step, 1)

                return {1: gather_sums, 2: invert, 3: residual_high, 4: residual_low, 5: statistics, 6: moments,
                        7: variance, 9: scale_rows}

            def block_weights(b, steps):
                for g in range(NG):
                    if g % CG == 0:
                        spread(b, g // CG)
                    make_weights(b, g)
                    if g % CG:
                        make_low(b, g - 1)
                    if g % CG == CG - 1:
                        make_low(b, g)
                    if g in steps:
                        steps[g]()

            block_weights(0, {})
            with dve.Fori(1, NB) as b:
                block_weights(b, finish(b - 1))
            for step in finish(NB - 1).values():
                step()


def kernel(**inputs):
    import concourse.bacc as bacc
    from concourse.bass_utils import run_bass_kernel_spmd

    nc = bacc.Bacc("TRN2", target_bir_lowering=False, num_devices=1)
    row = np.arange(P)
    arrays = {"in_ident": np.eye(P, dtype=np.float32),
              "in_powers": np.where(row[:, None] % WPT == np.arange(WPT)[None, :],
                               2.0 ** (row[:, None] // WPT), 0.0).astype(np.float32)}
    names = ["x", "adj", "L0_gnn_inlayer2", "L0_gnn_W1", "L0_gnn_w2", "L0_gnn_b2", "L0_gnn_w3", "L0_gnn_b3",
             "L1_gnn_beta"]
    for name in names:
        a = np.asarray(inputs[name])
        arrays["in_" + name] = np.ascontiguousarray(a.reshape(1, 1) if a.ndim == 0 else a)

    def dram(name):
        a = arrays[name]
        return nc.dram_tensor(name, a.shape, mybir.dt.from_np(a.dtype), kind="ExternalInput").ap()

    aps = [dram("in_" + name) for name in names]
    out = nc.dram_tensor("out", (N, D), F32, kind="ExternalOutput").ap()
    build_program(nc, *aps, dram("in_ident"), dram("in_powers"), out)
    r = run_bass_kernel_spmd(nc, [arrays], core_ids=[0])
    return r.results[0]["out"]
```

```python
from contextlib import ExitStack

import numpy as np

import concourse.bass as bass
from concourse import mybir

F32 = mybir.dt.float32
BF16 = mybir.dt.bfloat16
F16 = mybir.dt.float16
U16 = mybir.dt.uint16
U8 = mybir.dt.uint8
ALU = mybir.AluOpType
ACT = mybir.ActivationFunctionType
AX_X = mybir.AxisListType.X
ds = bass.ds

P = 128
N = 8192
D = 128
E2 = 256
JT = N // P
BLK = 512
NB = N // BLK
TB = BLK // P
GJ = 2
NG = JT // GJ
GW = GJ * BLK
CJ = 16
NC = JT // CJ
CG = CJ // GJ
BITS = 16
WPT = P // BITS
WB = BLK // BITS
SJ = 4
NS = JT // SJ
XA = D + 1
M0 = 4 * XA
M1 = 264
ONE = 7
HI = 8
LO = HI + D
M1N = M1 - ONE
PC = 8
SLOPE = 0.01
EPS = 1e-5
COS_EPS = 1e-7
BIG = 2.0 ** 100
TINY = 2.0 ** -100
XS = 32.0
MR = 4
AHEAD = 4
E0 = 12
E1 = 7


def wait(eng, sem, value):
    if isinstance(value, int) and value <= 0:
        return
    eng.wait_ge(sem, value)


def build_program(nc, x, adj, in2, w1, w2, b2, w3, b3, beta, ident_d, powers_d, out):
    x_rows = x.rearrange("(t p) d -> p t d", p=P)
    in2_rows = in2.rearrange("(t p) e -> p t e", p=P)
    out_rows = out.rearrange("(t p) d -> p t d", p=P)
    adj_rows = adj.rearrange("(b p t) c -> b p t c", p=P, t=TB)
    f1_dram = nc.dram_tensor("f1_scratch", (JT, P), F32, kind="Internal").ap()
    f1_blocks = f1_dram.rearrange("(b t) p -> b (t p)", t=TB)
    xs_dram = nc.dram_tensor("x1_scratch", (N, 4 * D), F16, kind="Internal").ap()
    xs_rows = xs_dram.rearrange("(t p) d -> p t d", p=P)

    with ExitStack() as whole:
        def keep(name, shape, dtype):
            return whole.enter_context(nc.sbuf_tensor(name, shape, dtype))

        bits = keep("bits", [P, NB * JT * WB], U16)
        ident16 = keep("ident16", [P, P], F16)
        ones16 = keep("ones16", [P, P], BF16)
        mhalf = keep("mhalf", [P, TB], F32)
        beta_scale = keep("beta_scale", [P, 1], F32)
        beta_shift = keep("beta_shift", [P, 1], F32)

        with ExitStack() as first:
            def sb(name, shape, dtype):
                return first.enter_context(nc.sbuf_tensor(name, shape, dtype))

            t = dict(
                mov=sb("mov0", [P, JT, M0], BF16),
                f2big=sb("f2big", [P, JT], F32),
                alpha=sb("alpha", [P, JT], F32),
                gamma=sb("gamma", [P, JT], F32),
                powers=sb("powers", [P, WPT], BF16),
                stage=sb("stage", [P, 2 * TB * SJ * P], F32),
                words=first.enter_context(nc.psum_tensor("words", [P, 2, 512], F32)),
                s_adj=[first.enter_context(nc.semaphore(name)) for name in ("s_adj_a", "s_adj_b")],
                s_read=first.enter_context(nc.semaphore("s_read")),
                s_bits=first.enter_context(nc.semaphore("s_bits")),
                tiny_hi=sb("tiny_hi0", [1, 2 * XA], BF16),
                tiny_lo=sb("tiny_lo0", [1, 2 * XA], BF16),
            )
            prepare(nc, adj_rows, bits, x_rows, in2_rows, w1, w2, b2, w3, b3, beta, ident_d, powers_d, f1_dram,
                    ident16, ones16, mhalf, beta_scale, beta_shift, t)
            layer0(nc, adj_rows, x_rows, f1_blocks, xs_rows, bits, ones16, mhalf, t)
        layer1(nc, xs_rows, out_rows, bits, ident16, ones16, mhalf, beta_scale, beta_shift)


def load_adj(nc, sp, t, adj_rows, b, c):
    s = c % 2
    wait(sp, t["s_read"], b * NS + (c - 1))
    sp.dma_start(t["stage"][:, s * TB * SJ * P:(s + 1) * TB * SJ * P].rearrange("p (t c) -> p t c", t=TB),
                 adj_rows[b, :, :, c * SJ * P:(c + 1) * SJ * P]).then_inc(t["s_adj"][s], 16)


def pack_load(nc, pe, t, b, c2, q):
    s, chunk = q % 2, q // (NS // NC)
    stage16 = t["stage"][:, :].bitcast(BF16)
    pe.wait_ge(t["s_adj"][s], (b * (NS // 2) + c2 * (NS // 4) + q // 2 + 1) * 16)
    if q % (NS // NC) == 0:
        wait(pe, t["s_bits"], b * NC + c2 * 2 + chunk - 1)
    for j in range(SJ):
        for i in range(TB):
            at = 2 * (((s * TB + i) * SJ + j) * P)
            col = ((q % (NS // NC)) * SJ + j) * WB + i * WPT
            mm = nc.tensor.matmul(t["words"][:, chunk, col:col + WPT], stage16[:, at + 1:at + 2 * P:2],
                                  t["powers"][:, :], start=True, stop=True, skip_group_check=True)
    mm.then_inc(t["s_read"], 1)


def take_words(nc, act, t, bits, b, c):
    act.wait_ge(t["s_read"], (b * NC + c + 1) * (NS // NC))
    nc.scalar.activation(
        bits[:, ds((b * NC + c) * CJ * WB, CJ * WB)].rearrange("p (j g t) -> p j g t", t=TB, g=WPT),
        t["words"][:, c % 2, :].rearrange("p (j t g) -> p j g t", t=TB, g=WPT), ACT.Copy).then_inc(t["s_bits"], 1)


def prepare(nc, adj_rows, bits, x_rows, in2_rows, w1, w2, b2, w3, b3, beta, ident_d, powers_d, f1_dram,
            ident16, ones16, mhalf, beta_scale, beta_shift, t):
    mov, f2big, alpha, gamma = t["mov"], t["f2big"], t["alpha"], t["gamma"]
    tiny_hi, tiny_lo = t["tiny_hi"], t["tiny_lo"]
    STEPS = JT // PC
    with ExitStack() as ctx:
        def sb(name, shape, dtype):
            return ctx.enter_context(nc.sbuf_tensor(name, shape, dtype))

        def sem(name):
            return ctx.enter_context(nc.semaphore(name))

        ident = sb("ident", [P, P], F32)
        powers32 = sb("powers32", [P, WPT], F32)
        ones32 = sb("ones32", [P, P], F32)
        w1_sb = sb("w1_sb", [P, E2], F32)
        w_col = sb("w_col", [P, 2], F32)
        w_rep = sb("w_rep", [P, 2, P], F32)
        row3 = sb("row3", [1, 3], F32)
        v = sb("v", [P, 2, E2], F32)
        cols3 = sb("cols3", [P, 3], F32)
        in2_ring = sb("in2_ring", [P, 2, PC, E2], F32)
        product = sb("product", [P, 2, E2], F32)
        f_step = sb("f_step", [P, 2, PC], F32)
        f1 = sb("f1", [P, JT], F32)
        f2 = sb("f2", [P, JT], F32)
        small = sb("small", [P, JT], F32)
        row_max = sb("row_max", [P, JT], F32)
        za = sb("za", [P, JT], F32)
        zg = sb("zg", [P, JT], F32)
        mx = sb("mx", [P, 1], F32)
        mx_one = sb("mx_one", [1, 1], F32)
        mx_all = sb("mx_all", [P, 1], F32)
        b_col = sb("b_col", [P, JT], F32)
        d_col = sb("d_col", [P, JT], F32)
        x_ring = sb("x_ring", [P, 2, PC, XA], F32)
        wx = sb("wx", [P, 2, PC, XA], F32)
        f1t = sb("f1t", [JT, P], F32)
        tiny32 = sb("tiny32", [1, 2 * XA], F32)
        ps_v = ctx.enter_context(nc.psum_tensor("ps_v", [P, 2 * E2], F32))
        ps_c = ctx.enter_context(nc.psum_tensor("ps_c", [P, 512], F32))
        ps_f = ctx.enter_context(nc.psum_tensor("ps_f", [P, 512], F32))
        ps_m = ctx.enter_context(nc.psum_tensor("ps_m", [P, 512], F32))
        ps_s = ctx.enter_context(nc.psum_tensor("ps_s", [P, 512], F32))

        s_const = sem("s_const")
        s_in2 = [sem("s_in2a"), sem("s_in2b")]
        s_xin = [sem("s_xina"), sem("s_xinb")]
        s_ones = sem("s_ones")
        s_rep = sem("s_rep")
        s_v = sem("s_v")
        s_vsb = sem("s_vsb")
        s_ttr = sem("s_ttr")
        s_f = sem("s_f")
        s_mx = sem("s_mx")
        s_mrow = sem("s_mrow")
        s_chain = sem("s_chain")
        s_exp = sem("s_exp")
        s_f1t = sem("s_f1t")
        s_f1sb = sem("s_f1sb")
        s_f1out = sem("s_f1out")
        s_wx = sem("s_wx")
        s_hi = sem("s_hi")
        s_lo = sem("s_lo")
        s_cs = sem("s_cs")
        s_end = sem("s_end")
        block = ctx.enter_context(nc.Block())

        @block.sync
        def _(sp):
            loads = [(ident[:, :], ident_d), (powers32[:, :], powers_d), (w1_sb[:, :], w1),
                     (w_col[:, 0:1], w2.rearrange("(h o) -> h o", o=1)),
                     (w_col[:, 1:2], w3.rearrange("(h o) -> h o", o=1)),
                     (row3[:, 0:1], b2), (row3[:, 1:2], b3),
                     (row3[:, 2:3], beta.rearrange("(a b) -> a b", a=1))]
            for dst, src in loads:
                sp.dma_start(dst, src).then_inc(s_const, 16)
            for c in range(NS):
                load_adj(nc, sp, t, adj_rows, 0, c)
            for c in range(2):
                load_adj(nc, sp, t, adj_rows, 1, c)
            sp.wait_ge(s_f1sb, 1)
            sp.dma_start(f1_dram, f1t[:, :]).then_inc(s_f1out, 16)
            sp.wait_ge(s_f1out, 16)

        @block.tensor
        def _(pe):
            pe.wait_ge(s_ones, 3)
            pe.wait_ge(s_rep, 2)
            pe.wait_ge(s_const, 16 * 8)
            for w in range(2):
                mm = nc.tensor.matmul(ps_v[:, w * E2:(w + 1) * E2], w_rep[:, w, :], w1_sb[:, :], start=True, stop=True)
            mm = nc.tensor.matmul(ps_c[:, 0:3], ones32[0:1, :], row3[:, :], start=True, stop=True)
            mm.then_inc(s_v, 1)
            nc.tensor.matmul(ps_f[:, 0:1], ones32[0:1, :], ones32[0:1, 0:1], start=True, stop=True).then_inc(s_cs, 2)

            def pack(load):
                pack_load(nc, pe, t, 0, load // (NS // 2), load % (NS // 2))

            for load in range(STEPS):
                pack(load)
            pe.wait_ge(s_mx, 1)
            nc.tensor.transpose(ps_m[0:1, 0:P], mx[:, :], ident[:, :]).then_inc(s_mrow, 1)
            pe.wait_ge(s_mx, 2)
            nc.tensor.matmul(ps_m[:, P:P + 1], ones32[0:1, :], mx_one[:, :], start=True, stop=True,
                             skip_group_check=True).then_inc(s_mrow, 1)
            pe.wait_ge(s_chain, 3)
            nc.tensor.transpose(ps_f[0:JT, 0:P], f1[:, :], ident[:, :]).then_inc(s_f1t, 1)
            for k in range(STEPS):
                pack(NS - STEPS + k)
                pe.wait_ge(s_xin[k % 2], (k // 2 + 1) * 16)
                pe.wait_ge(s_wx, k * 2 + 2)
                for j in range(PC):
                    mm = nc.tensor.matmul(ps_s[0:1, 0:XA], ones32[:, 0:1], x_ring[:, k % 2, j, :],
                                          start=False, stop=False, skip_group_check=True)
                mm.then_inc(s_cs, 1)

        @block.gpsimd
        def _(pool):
            nc.gpsimd.memset(mhalf[:, :], -0.5)
            for k in range(STEPS):
                pool.wait_ge(s_f, k + 1)
                pool.dma_start(in2_ring[:, k % 2, :, :], in2_rows[:, k * PC:(k + 1) * PC, :]).then_inc(s_in2[k % 2], 16)
            for k in range(STEPS):
                pool.wait_ge(s_cs, k + 1)
                pool.dma_start(x_ring[:, k % 2, :, 0:D], x_rows[:, k * PC:(k + 1) * PC, :]).then_inc(s_xin[k % 2], 16)

        @block.scalar
        def _(act):
            act.wait_ge(s_v, 1)
            nc.scalar.activation(v[:, :, :], ps_v[:, :].rearrange("p (w e) -> p w e", w=2), ACT.Copy)
            nc.scalar.activation(cols3[:, :], ps_c[:, 0:3], ACT.Copy).then_inc(s_vsb, 1)
            take_words(nc, act, t, bits, 0, 0)
            take_words(nc, act, t, bits, 0, 1)
            act.wait_ge(s_chain, 1)
            nc.scalar.activation(b_col[:, :], f2[:, :], ACT.Exp)
            nc.scalar.activation(d_col[:, :], f2[:, :], ACT.Exp, scale=SLOPE).then_inc(s_exp, 1)
            act.wait_ge(s_chain, 7)
            nc.scalar.activation(alpha[:, :], za[:, :], ACT.Exp)
            nc.scalar.activation(gamma[:, :], zg[:, :], ACT.Exp).then_inc(s_exp, 1)
            act.wait_ge(s_vsb, 1)
            nc.scalar.activation(beta_scale[:, :], cols3[:, 2:3], ACT.Copy, scale=1.0 / (XS * XS))
            for k in range(STEPS):
                if k == STEPS // 2:
                    take_words(nc, act, t, bits, 0, 2)
                for w in range(2):
                    act.wait_ge(s_wx, k * 2 + w + 1)
                    nc.scalar.activation(mov[:, ds(k * PC, PC), 2 * w * XA:(2 * w + 1) * XA], wx[:, w, :, :],
                                         ACT.Copy).then_inc(s_hi, 1)

        @block.vector
        def _(dve):
            links = [0]

            def chain(instruction):
                links[0] += 1
                instruction.then_inc(s_chain, 1)
                dve.wait_ge(s_chain, links[0])

            nc.vector.memset(ones16[:, :], 1.0)
            nc.vector.memset(x_ring[:, :, :, D:XA], 1.0)
            nc.vector.memset(ps_s[:, :], 0.0).then_inc(s_ones, 1)
            nc.vector.memset(tiny32[:, :], 0.0).then_inc(s_ones, 1)
            nc.vector.memset(ones32[:, :], 1.0).then_inc(s_ones, 1)
            dve.wait_ge(s_ones, 3)
            nc.vector.memset(small[:, 0:1], 0.0).then_inc(s_f, 2)
            dve.wait_ge(s_const, 16 * 8)
            nc.vector.tensor_copy(ident16[:, :], ident[:, :])
            nc.vector.tensor_copy(t["powers"][:, :], powers32[:, :])
            for w in range(2):
                nc.vector.tensor_scalar(w_rep[:, w, :], ones32[:, :], w_col[:, w:w + 1], None, ALU.mult).then_inc(s_rep, 1)
            dve.wait_ge(s_vsb, 1)
            with dve.Fori(0, STEPS // 2) as n:
                for s in range(2):
                    k = n * 2 + s
                    dve.wait_ge(s_in2[s], n * 16 + 16)
                    for j in range(PC):
                        for w in range(2):
                            c = j * 2 + w
                            if c >= 2:
                                dve.wait_ge(s_ttr, k * 2 * PC + c - 1)
                            elif c == 0:
                                dve.wait_ge(s_f, k + 2)
                            nc.vector.tensor_tensor_reduce(
                                product[:, w, :], in2_ring[:, s, j, :], v[:, w, :], 1.0, 0.0, ALU.mult, ALU.add,
                                f_step[:, w, j:j + 1]).then_inc(s_ttr, 1)
                    dve.wait_ge(s_ttr, (k + 1) * 2 * PC)
                    nc.vector.tensor_copy(f1[:, ds(k * PC, PC)], f_step[:, 0, :])
                    nc.vector.tensor_copy(f2[:, ds(k * PC, PC)], f_step[:, 1, :]).then_inc(s_f, 1)
            dve.wait_ge(s_f, STEPS + 2)
            nc.vector.reduce_max(mx[:, :], f2[:, :], AX_X).then_inc(s_mx, 1)
            dve.wait_ge(s_mrow, 1)
            nc.vector.reduce_max(mx_one[:, :], ps_m[0:1, 0:P], AX_X).then_inc(s_mx, 1)
            dve.wait_ge(s_mrow, 2)
            nc.vector.tensor_copy(mx_all[:, :], ps_m[:, P:P + 1]).then_inc(s_mx, 1)
            dve.wait_ge(s_mx, 3)
            chain(nc.vector.tensor_scalar(f2[:, :], f2[:, :], mx_all[:, 0:1], None, ALU.subtract))
            chain(nc.vector.tensor_scalar(f1[:, :], f1[:, :], cols3[:, 0:1], cols3[:, 1:2], ALU.add, ALU.add))
            chain(nc.vector.tensor_scalar(f1[:, :], f1[:, :], mx_all[:, 0:1], None, ALU.add))
            chain(nc.vector.tensor_scalar(small[:, :], f1[:, :], SLOPE, None, ALU.mult))
            chain(nc.vector.tensor_tensor(row_max[:, :], f1[:, :], small[:, :], ALU.max))
            chain(nc.vector.tensor_tensor(za[:, :], f1[:, :], row_max[:, :], ALU.subtract))
            chain(nc.vector.tensor_tensor(zg[:, :], small[:, :], row_max[:, :], ALU.subtract))
            chain(nc.vector.tensor_scalar(f2big[:, :], f2[:, :], BIG, None, ALU.mult))
            chain(nc.vector.tensor_scalar(beta_shift[:, :], cols3[:, 2:3], -1.0, None, ALU.mult))
            chain(nc.vector.tensor_tensor(beta_shift[:, :], beta_shift[:, :], cols3[:, 2:3], ALU.min))
            dve.wait_ge(s_exp, 1)
            with dve.Fori(0, STEPS // 2) as n:
                for s in range(2):
                    k = n * 2 + s
                    dve.wait_ge(s_xin[s], n * 16 + 16)
                    for w, factor in enumerate((b_col, d_col)):
                        nc.vector.tensor_tensor(
                            wx[:, w, :, :], x_ring[:, s, :, :],
                            factor[:, ds(k * PC, PC)].unsqueeze(2).to_broadcast([P, PC, XA]), ALU.mult).then_inc(s_wx, 1)
                    for w in range(2):
                        dve.wait_ge(s_hi, k * 2 + w + 1)
                        nc.vector.tensor_tensor(
                            mov[:, ds(k * PC, PC), (2 * w + 1) * XA:(2 * w + 2) * XA], wx[:, w, :, :],
                            mov[:, ds(k * PC, PC), 2 * w * XA:(2 * w + 1) * XA], ALU.subtract).then_inc(s_lo, 1)
                    dve.wait_ge(s_lo, k * 2 + 2)
            dve.wait_ge(s_f1t, 1)
            nc.vector.tensor_copy(f1t[:, :], ps_f[0:JT, 0:P]).then_inc(s_f1sb, 1)
            dve.wait_ge(s_cs, STEPS + 2)
            chain(nc.vector.tensor_scalar(tiny32[:, XA:2 * XA], ps_s[0:1, 0:XA], TINY, None, ALU.mult))
            chain(nc.vector.tensor_copy(tiny_hi[:, :], tiny32[:, :]))
            nc.vector.tensor_tensor(tiny_lo[:, :], tiny32[:, :], tiny_hi[:, :], ALU.subtract).then_inc(s_end, 1)


def norm_rows(nc, dve, s_step, done, rows, stats, mv, ve):
    def statistics():
        dve.wait_ge(s_step, done)
        for i in range(TB):
            ins = nc.vector.bn_stats(stats[:, i, :], rows[:, i, :])
        ins.then_inc(s_step, 1)

    def moments():
        dve.wait_ge(s_step, done + 1)
        nc.vector.memset(ve[:, :], 0.0)
        for i in range(TB):
            ins = nc.vector.bn_aggr(mv[:, i, :], stats[:, i, :])
        ins.then_inc(s_step, 1)

    def variance():
        dve.wait_ge(s_step, done + 2)
        nc.vector.tensor_scalar(ve[:, :], mv[:, :, 1], EPS, None, ALU.add).then_inc(s_step, 1)

    return statistics, moments, variance


def chunk_words(bits, b, c):
    return bits[:, ds((b * NC + c) * CJ * WB, CJ * WB)].rearrange("p (j w) -> p j w", w=WB)


def layer0(nc, adj_rows, x_rows, f1_blocks, xs_rows, bits, ones16, mhalf, t):
    mov, f2big, alpha, gamma = t["mov"], t["f2big"], t["alpha"], t["gamma"]
    tiny_hi, tiny_lo = t["tiny_hi"], t["tiny_lo"]
    s_bits = t["s_bits"]
    with ExitStack() as ctx:
        def sb(name, shape, dtype):
            return ctx.enter_context(nc.sbuf_tensor(name, shape, dtype))

        def sem(name):
            return ctx.enter_context(nc.semaphore(name))

        mask = sb("mask0", [P, CJ * BLK], U16)
        side = sb("side", [P, 2, GW], BF16)
        upper = sb("upper", [P, MR, GJ, BLK], BF16)
        lower = sb("lower", [P, MR, GJ, BLK], BF16)
        f1_row = sb("f1_row", [P, BLK], F32)
        x_blk = sb("x_blk", [P, TB, D], F32)
        part = sb("part0", [P, TB, XA], F32)
        sums = sb("sums0", [P, TB, XA], F32)
        y = sb("y0", [P, TB, D], F32)
        x1 = sb("x1", [P, TB, D], F32)
        x1_out = sb("x1_out", [P, TB, 4 * D], F16)
        inv = sb("inv0", [P, TB], F32)
        stats = sb("stats0", [P, TB, 6], F32)
        mv = sb("mv0", [P, TB, 2], F32)
        ve = sb("ve0", [P, TB], F32)
        rstd = sb("rstd0", [P, TB], F32)
        n2 = sb("n2", [P, TB], F32)
        rnorm = sb("rnorm", [P, TB], F32)
        acc = ctx.enter_context(nc.psum_tensor("acc0", [P, TB, 512], F32))
        mask16 = mask[:, :].bitcast(BF16)

        s_f1row = sem("s_f1row")
        s_side = sem("s_side")
        s_mask = sem("s_mask")
        s_upper = sem("s_upper")
        s_lower = sem("s_lower")
        s_used = sem("s_used")
        s_part = sem("s_part")
        s_open = sem("s_open0")
        s_step = sem("s_step0")
        s_x = sem("s_x")
        s_pow = sem("s_pow0")
        s_rn = sem("s_rn")
        s_hi = sem("s_hi0")
        s_st = sem("s_st")
        block = ctx.enter_context(nc.Block())

        @block.sync
        def _(sp):
            def load_f1(b):
                wait(sp, s_side, b * NG)
                sp.dma_start(f1_row[:, :], f1_blocks[ds(b, 1), :].broadcast_to([P, BLK])).then_inc(s_f1row, 16)

            def load_x(b):
                wait(sp, s_step, (b - 1) * E0 + 2)
                sp.dma_start(x_blk[:, :, :], x_rows[:, ds(b * TB, TB), :]).then_inc(s_x, 16)

            def store_x1(b):
                sp.wait_ge(s_step, (b + 1) * E0)
                sp.dma_start(xs_rows[:, ds(b * TB, TB), :], x1_out[:, :, :]).then_inc(s_st, 16)

            load_f1(0)
            for c in range(2, NS // 2):
                load_adj(nc, sp, t, adj_rows, 1, c)
            load_x(0)
            for c in range(NS // 2, NS):
                load_adj(nc, sp, t, adj_rows, 1, c)
            with sp.Fori(1, NB - 1) as b:
                load_f1(b)
                for c in range(NS):
                    load_adj(nc, sp, t, adj_rows, b + 1, c)
                    if c == NS - 3:
                        store_x1(b - 1)
                        load_x(b)
            load_f1(NB - 1)
            store_x1(NB - 2)
            load_x(NB - 1)
            store_x1(NB - 1)
            sp.wait_ge(s_st, 16 * (NB + 1))

        @block.tensor
        def _(pe):
            def block_sums(b, packs):
                for i in range(TB):
                    pe.wait_ge(s_open, b * TB + i + 1)
                    for n, row in enumerate((tiny_hi, tiny_lo)):
                        nc.tensor.matmul(acc[:, i, 0:2 * XA], ones16[0:1, :], row[:, :],
                                         start=(n == 0), stop=False, skip_group_check=True)
                with pe.Fori(0, 2) as c2:
                    for g in range(NG // 2):
                        pe.wait_ge(s_lower, b * NG + c2 * (NG // 2) + g + 1)
                        for j in range(GJ):
                            for i in range(TB):
                                for w, weights in enumerate((upper, lower)):
                                    for half in range(2):
                                        at = (2 * w + half) * XA
                                        mm = nc.tensor.matmul(
                                            acc[:, i, w * XA:(w + 1) * XA],
                                            weights[:, g % MR, j, i * P:(i + 1) * P],
                                            mov[:, c2 * (JT // 2) + g * GJ + j, at:at + XA],
                                            start=False, stop=False, skip_group_check=True)
                        mm.then_inc(s_used, 1)
                        if packs and g % 2 == 1:
                            pack_load(nc, pe, t, b + 1, c2, g // 2)

            with pe.Fori(0, NB - 1) as b:
                block_sums(b, True)
            block_sums(NB - 1, False)

        @block.scalar
        def _(act):
            def finish_part(b):
                act.wait_ge(s_used, (b + 1) * NG)
                act.wait_ge(s_open, (b + 1) * TB)
                for i in range(TB):
                    nc.scalar.activation(part[:, i, :], acc[:, i, XA:2 * XA], ACT.Copy,
                                         scale=gamma[:, ds(b * TB + i, 1)]).then_inc(s_part, 1)

            def finish_x1_high(b):
                act.wait_ge(s_step, b * E0 + 6)
                act.wait_ge(s_st, b * 16 + 16)
                nc.scalar.activation(x1_out[:, :, 0:D], x1[:, :, :], ACT.Copy).then_inc(s_hi, 1)

            def finish_xn_high(b):
                act.wait_ge(s_step, b * E0 + 10)
                nc.scalar.activation(x1_out[:, :, 2 * D:3 * D], y[:, :, :], ACT.Copy).then_inc(s_hi, 1)

            def block_sides(b, finish, packs):
                act.wait_ge(s_f1row, (b + 1) * 16)
                for g in range(NG):
                    wait(act, s_upper, b * NG + g - 1)
                    for j in range(GJ):
                        jt = g * GJ + j
                        ins = nc.scalar.activation(side[:, g % 2, j * BLK:(j + 1) * BLK], f1_row[:, :], ACT.Relu,
                                                   bias=f2big[:, jt:jt + 1], scale=BIG)
                    ins.then_inc(s_side, 1)
                    if g == CG - 1:
                        take_words(nc, act, t, bits, b, NC - 1)
                    elif packs and g % CG == CG - 1:
                        take_words(nc, act, t, bits, b + 1, g // CG - 1)
                    if finish:
                        if g == 3:
                            finish_part(b - 1)
                        if g == 11:
                            finish_x1_high(b - 1)
                        if g == 15:
                            finish_xn_high(b - 1)

            block_sides(0, False, True)
            with act.Fori(1, NB - 1) as b:
                block_sides(b, True, True)
            block_sides(NB - 1, True, False)
            finish_part(NB - 1)
            finish_x1_high(NB - 1)
            finish_xn_high(NB - 1)

        @block.gpsimd
        def _(pool):
            with pool.Fori(0, NB) as b:
                pool.wait_ge(s_step, b * E0 + 5)
                nc.gpsimd.tensor_tensor(rstd[:, :], ve[:, :], mhalf[:, :], ALU.pow).then_inc(s_pow, 1)
                pool.wait_ge(s_step, b * E0 + 9)
                nc.gpsimd.tensor_tensor(rnorm[:, :], n2[:, :], mhalf[:, :], ALU.pow).then_inc(s_rn, 1)

        @block.vector
        def _(dve):
            def spread(b, c):
                wait(dve, s_lower, b * NG + c * CG)
                dve.wait_ge(s_bits, b * NC + c + 1)
                source = chunk_words(bits, b, c)
                target = mask[:, :].rearrange("p (j k w) -> p j k w", k=BITS, w=WB)
                for k in range(BITS):
                    shift, op = (14 - k, ALU.logical_shift_left) if k < 15 else (1, ALU.logical_shift_right)
                    ins = nc.vector.tensor_scalar(target[:, :, k, :], source, shift, 0x4000, op, ALU.bitwise_and)
                ins.then_inc(s_mask, 1)

            def make_upper(b, g):
                m = (g % CG) * GW
                dve.wait_ge(s_side, b * NG + g + 1)
                if g % CG == 0:
                    dve.wait_ge(s_mask, b * NC + g // CG + 1)
                wait(dve, s_used, b * NG + g + 1 - MR)
                nc.vector.tensor_tensor(upper[:, g % MR, :, :].rearrange("p j i -> p (j i)"), side[:, g % 2, :],
                                        mask16[:, m:m + GW], ALU.min).then_inc(s_upper, 1)

            def make_lower(b, g):
                m = (g % CG) * GW
                dve.wait_ge(s_upper, b * NG + g + 1)
                nc.vector.tensor_tensor(lower[:, g % MR, :, :].rearrange("p j i -> p (j i)"), mask16[:, m:m + GW],
                                        upper[:, g % MR, :, :].rearrange("p j i -> p (j i)"),
                                        ALU.subtract).then_inc(s_lower, 1)

            def finish(b):
                base = b * E0

                def gather_sums():
                    for i in range(TB):
                        dve.wait_ge(s_part, b * TB + i + 1)
                        nc.vector.scalar_tensor_tensor(
                            out=sums[:, i, :], in0=acc[:, i, 0:XA], scalar=alpha[:, ds(b * TB + i, 1)],
                            in1=part[:, i, :], op0=ALU.mult, op1=ALU.add).then_inc(s_open, 1)

                def invert():
                    dve.wait_ge(s_open, (b + 2) * TB)
                    nc.vector.reciprocal(inv[:, :], sums[:, :, D]).then_inc(s_step, 1)

                def residual():
                    dve.wait_ge(s_step, base + 1)
                    dve.wait_ge(s_x, (b + 1) * 16)
                    for i in range(TB):
                        ins = nc.vector.scalar_tensor_tensor(
                            out=y[:, i, :], in0=sums[:, i, 0:D], scalar=inv[:, i:i + 1], in1=x_blk[:, i, :],
                            op0=ALU.mult, op1=ALU.add)
                    ins.then_inc(s_step, 1)

                statistics, moments, variance = norm_rows(nc, dve, s_step, base + 2, y, stats, mv, ve)

                def scale_rows():
                    dve.wait_ge(s_pow, b + 1)
                    for i in range(TB):
                        ins = nc.vector.tensor_scalar(x1[:, i, :], y[:, i, :], mv[:, i, 0:1], rstd[:, i:i + 1],
                                                      ALU.subtract, ALU.mult)
                    ins.then_inc(s_step, 1)

                def norm_a():
                    nc.vector.tensor_tensor(n2[:, :], rstd[:, :], rstd[:, :], ALU.mult).then_inc(s_step, 1)

                def norm_b():
                    dve.wait_ge(s_step, base + 7)
                    nc.vector.tensor_tensor(n2[:, :], n2[:, :], mv[:, :, 1], ALU.mult).then_inc(s_step, 1)

                def norm_c():
                    dve.wait_ge(s_step, base + 8)
                    nc.vector.tensor_scalar(n2[:, :], n2[:, :], float(D), COS_EPS, ALU.mult, ALU.add)\
                        .then_inc(s_step, 1)

                def normed_rows():
                    dve.wait_ge(s_rn, b + 1)
                    for i in range(TB):
                        ins = nc.vector.tensor_scalar(y[:, i, :], x1[:, i, :], rnorm[:, i:i + 1], XS,
                                                      ALU.mult, ALU.mult)
                    ins.then_inc(s_step, 1)

                def x1_low():
                    dve.wait_ge(s_hi, b * 2 + 1)
                    nc.vector.tensor_tensor(x1_out[:, :, D:2 * D], x1[:, :, :], x1_out[:, :, 0:D],
                                            ALU.subtract).then_inc(s_step, 1)

                def xn_low():
                    dve.wait_ge(s_hi, b * 2 + 2)
                    nc.vector.tensor_tensor(x1_out[:, :, 3 * D:4 * D], y[:, :, :], x1_out[:, :, 2 * D:3 * D],
                                            ALU.subtract).then_inc(s_step, 1)

                return {1: gather_sums, 2: invert, 3: residual, 4: statistics, 5: moments, 6: variance,
                        8: scale_rows, 9: norm_a, 10: norm_b, 11: norm_c, 13: normed_rows, 14: x1_low, 18: xn_low}

            def block_masks(b, steps):
                for g in range(NG):
                    if g % CG == 0:
                        spread(b, g // CG)
                    make_upper(b, g)
                    if g % CG:
                        make_lower(b, g - 1)
                    if g % CG == CG - 1:
                        make_lower(b, g)
                    if g in steps:
                        steps[g]()

            nc.vector.memset(inv[:, :], 0.0).then_inc(s_open, TB)
            nc.vector.memset(n2[:, :], 0.0).then_inc(s_st, 16)
            block_masks(0, {})
            with dve.Fori(1, NB) as b:
                block_masks(b, finish(b - 1))
            for step in finish(NB - 1).values():
                step()


def layer1(nc, xs_rows, out_rows, bits, ident16, ones16, mhalf, beta_scale, beta_shift):
    TT = 4
    TL = 2 * TT
    LS = 4
    with ExitStack() as ctx:
        def sb(name, shape, dtype):
            return ctx.enter_context(nc.sbuf_tensor(name, shape, dtype))

        def sem(name):
            return ctx.enter_context(nc.semaphore(name))

        mov = sb("mov1", [P, JT, M1], F16)
        xnt = sb("xnt", [P, 2, N], F16)
        mask = sb("mask1", [P, CJ * BLK // 2], U16)
        exps = sb("exps", [P, 2, GW], F32)
        wts = sb("wts", [P, MR * GW], F32)
        low = sb("low", [P, MR, GJ, BLK], BF16)
        tiny32 = sb("tiny32b", [1, M1N], F32)
        tiny_hi = sb("tiny_hi1", [1, M1N], BF16)
        tiny_lo = sb("tiny_lo1", [1, M1N], BF16)
        part = sb("part1", [P, TB, XA], F32)
        sums = sb("sums1", [P, TB, XA], F32)
        inv = sb("inv1", [P, TB], F32)
        y = sb("y1", [P, TB, D], F32)
        result = sb("result", [P, TB, D], F32)
        stats = sb("stats1", [P, TB, 6], F32)
        mv = sb("mv1", [P, TB, 2], F32)
        ve = sb("ve1", [P, TB], F32)
        rstd = sb("rstd1", [P, TB], F32)
        acc = ctx.enter_context(nc.psum_tensor("acc1", [P, TB, 512], F32))
        scores = ctx.enter_context(nc.psum_tensor("scores", [P, 2, GJ, BLK], F32))
        mask8 = mask[:, :].bitcast(U8)
        wts_hi = wts[:, :].bitcast(BF16)
        xn_in = wts[:, :].bitcast(F16).rearrange("p (t d) -> p t d", d=2 * D)

        s_mov = sem("s_mov")
        s_one = sem("s_one")
        s_xn = [sem(f"s_xn_{k}") for k in range(LS)]
        s_turn = sem("s_turn")
        s_thi = sem("s_thi")
        s_tlo = sem("s_tlo")
        s_cs = sem("s_cs1")
        s_tiny = sem("s_tiny")
        s_scores = sem("s_scores")
        s_exps = sem("s_exps")
        s_mask = sem("s_mask1")
        s_wts = sem("s_wts")
        s_low = sem("s_low")
        s_used = sem("s_used1")
        s_part = sem("s_part1")
        s_open = sem("s_open1")
        s_step = sem("s_step1")
        s_pow = sem("s_pow1")
        s_st = sem("s_st1")
        block = ctx.enter_context(nc.Block())

        @block.sync
        def _(sp):
            for k in range(JT // TL):
                wait(sp, s_turn, 2 * (k - LS + 1))
                at = k % LS * TL
                sp.dma_start(xn_in[:, at:at + TL, :], xs_rows[:, k * TL:(k + 1) * TL, 2 * D:4 * D])\
                    .then_inc(s_xn[k % LS], 16)
            for k in range(JT // PC):
                sp.dma_start(mov[:, k * PC:(k + 1) * PC, HI:M1],
                             xs_rows[:, k * PC:(k + 1) * PC, 0:2 * D]).then_inc(s_mov, 16)

            def store(b):
                sp.wait_ge(s_step, (b + 1) * E1)
                sp.dma_start(out_rows[:, ds(b * TB, TB), :], result[:, :, :]).then_inc(s_st, 16)

            with sp.Fori(0, NB) as b:
                store(b)
            sp.wait_ge(s_st, 16 * (NB + 1))

        @block.tensor
        def _(pe):
            for k in range(JT // TT):
                load = k // 2
                if k % 2 == 0:
                    pe.wait_ge(s_xn[load % LS], (load // LS + 1) * 16)
                wait(pe, s_thi, k - 1)
                wait(pe, s_tlo, k - 1)
                for half in range(2):
                    for i in range(TT):
                        mm = nc.tensor.matmul(scores[:, k % 2, half, i * P:(i + 1) * P],
                                              xn_in[:, load % LS * TL + k % 2 * TT + i, half * D:(half + 1) * D], ident16[:, :],
                                              start=True, stop=True, skip_group_check=True)
                mm.then_inc(s_turn, 1)
            pe.wait_ge(s_thi, JT // TT)
            pe.wait_ge(s_tlo, JT // TT)

            def make_scores(b, g, slot, n):
                wait(pe, s_exps, n - 1)
                for j in range(GJ):
                    for m, (left, right) in enumerate(((0, 0), (0, 1), (1, 0))):
                        mm = nc.tensor.matmul(scores[:, slot, j, :],
                                              xnt[:, left, ds((g * GJ + j) * P, P)],
                                              xnt[:, right, ds(b * BLK, BLK)],
                                              start=(m == 0), stop=(m == 2))
                mm.then_inc(s_scores, 1)

            def weigh(b, g, q):
                pe.wait_ge(s_low, b * NG + g + 1)
                for j in range(GJ):
                    for i in range(TB):
                        at = 2 * (((q % MR) * GJ + j) * BLK + i * P)
                        nc.tensor.matmul(acc[:, i, 0:M1N], wts_hi[:, at + 1:at + 2 * P:2],
                                         mov[:, g * GJ + j, ONE:M1], start=False, stop=False, skip_group_check=True)
                        mm = nc.tensor.matmul(acc[:, i, 0:XA], low[:, q % MR, j, i * P:(i + 1) * P],
                                              mov[:, g * GJ + j, ONE:LO], start=False, stop=False, skip_group_check=True)
                mm.then_inc(s_used, 1)

            def block_sums(b, last):
                def chunk(c, end):
                    for q in range(CG):
                        g = c * CG + q
                        weigh(b, g, q)
                        if not end or q < CG - AHEAD:
                            make_scores(b, g + AHEAD, (q + AHEAD) % 2, b * NG + g + AHEAD)
                        elif not last:
                            make_scores(b + 1, q - (CG - AHEAD), (q + AHEAD) % 2, b * NG + g + AHEAD)

                for i in range(TB):
                    pe.wait_ge(s_open, b * TB + i + 1)
                    for n, row in enumerate((tiny_hi, tiny_lo)):
                        nc.tensor.matmul(acc[:, i, 0:M1N], ones16[0:1, :], row[:, :],
                                         start=(n == 0), stop=False, skip_group_check=True)
                with pe.Fori(0, NC - 1) as c:
                    chunk(c, False)
                chunk(NC - 1, True)

            for g in range(AHEAD):
                make_scores(0, g, g % 2, g)
            pe.wait_ge(s_mov, 16 * (JT // PC))
            pe.wait_ge(s_one, 1)
            for j in range(JT):
                mm = nc.tensor.matmul(acc[0:1, 0, 0:M1N], ones16[:, 0:1], mov[:, j, ONE:M1],
                                      start=(j == 0), stop=(j == JT - 1))
            mm.then_inc(s_cs, 1)
            pe.wait_ge(s_tiny, 1)
            with pe.Fori(0, NB - 1) as b:
                block_sums(b, False)
            block_sums(NB - 1, True)

        @block.scalar
        def _(act):
            for k in range(JT // TT):
                act.wait_ge(s_turn, k + 1)
                nc.scalar.activation(xnt[:, 0, k * TT * P:(k + 1) * TT * P], scores[:, k % 2, 0, :],
                                     ACT.Copy).then_inc(s_thi, 1)

            def make_exps(b, g):
                act.wait_ge(s_scores, b * NG + g + 1)
                wait(act, s_wts, b * NG + g - 1)
                nc.scalar.activation(exps[:, g % 2, :], scores[:, g % 2, :, :].rearrange("p j i -> p (j i)"), ACT.Exp,
                                     bias=beta_shift[:, 0:1], scale=beta_scale[:, 0:1]).then_inc(s_exps, 1)

            def finish_part(b):
                act.wait_ge(s_used, (b + 1) * NG)
                act.wait_ge(s_open, (b + 1) * TB)
                for i in range(TB):
                    nc.scalar.activation(part[:, i, 1:XA], acc[:, i, XA:M1N], ACT.Copy).then_inc(s_part, 1)

            def block_exps(b, finish):
                for g in range(NG):
                    make_exps(b, g)
                    if finish and g == 1:
                        finish_part(b - 1)

            block_exps(0, False)
            with act.Fori(1, NB) as b:
                block_exps(b, True)
            finish_part(NB - 1)

        @block.gpsimd
        def _(pool):
            with pool.Fori(0, NB) as b:
                pool.wait_ge(s_step, b * E1 + 6)
                nc.gpsimd.tensor_tensor(rstd[:, :], ve[:, :], mhalf[:, :], ALU.pow).then_inc(s_pow, 1)

        @block.vector
        def _(dve):
            nc.vector.memset(mov[:, :, ONE:HI], 1.0).then_inc(s_one, 1)
            nc.vector.memset(part[:, :, 0:1], 0.0).then_inc(s_open, TB)
            nc.vector.memset(inv[:, :], 0.0).then_inc(s_st, 16)
            for k in range(JT // TT):
                dve.wait_ge(s_turn, k + 1)
                nc.vector.tensor_copy(xnt[:, 1, k * TT * P:(k + 1) * TT * P], scores[:, k % 2, 1, :]).then_inc(s_tlo, 1)
            dve.wait_ge(s_cs, 1)
            nc.vector.tensor_scalar(tiny32[:, :], acc[0:1, 0, 0:M1N], TINY, None, ALU.mult).then_inc(s_cs, 1)
            dve.wait_ge(s_cs, 2)
            nc.vector.tensor_copy(tiny_hi[:, :], tiny32[:, :]).then_inc(s_cs, 1)
            dve.wait_ge(s_cs, 3)
            nc.vector.tensor_tensor(tiny_lo[:, :], tiny32[:, :], tiny_hi[:, :], ALU.subtract).then_inc(s_tiny, 1)

            def spread(b, c):
                wait(dve, s_wts, b * NG + c * CG)
                source = chunk_words(bits, b, c)
                target = mask[:, :].rearrange("p (j k w) -> p j k w", k=BITS // 2, w=WB)
                for k in range(BITS // 2):
                    ins = nc.vector.tensor_scalar(target[:, :, k, :], source, k, 0x0101,
                                                  ALU.logical_shift_right, ALU.bitwise_and)
                ins.then_inc(s_mask, 1)

            def make_weights(b, g):
                m = (g % CG) * GW
                at = (g % MR) * GW
                dve.wait_ge(s_exps, b * NG + g + 1)
                if g % CG == 0:
                    dve.wait_ge(s_mask, b * NC + g // CG + 1)
                wait(dve, s_used, b * NG + g + 1 - MR)
                rows = "p (j h r) -> p j h r"
                nc.vector.tensor_tensor(wts[:, at:at + GW].rearrange(rows, j=GJ, h=2),
                                        exps[:, g % 2, :].rearrange(rows, j=GJ, h=2),
                                        mask8[:, m:m + GW].rearrange("p (j r h) -> p j h r", j=GJ, h=2),
                                        ALU.mult).then_inc(s_wts, 1)

            def make_low(b, g):
                at = (g % MR) * GW
                dve.wait_ge(s_wts, b * NG + g + 1)
                nc.vector.tensor_tensor(low[:, g % MR, :, :].rearrange("p j i -> p (j i)"), wts[:, at:at + GW],
                                        wts_hi[:, 2 * at + 1:2 * (at + GW):2], ALU.subtract).then_inc(s_low, 1)

            def finish(b):
                base = b * E1

                def gather_sums():
                    for i in range(TB):
                        dve.wait_ge(s_part, b * TB + i + 1)
                        nc.vector.tensor_tensor(sums[:, i, :], acc[:, i, 0:XA], part[:, i, :], ALU.add)\
                            .then_inc(s_open, 1)

                def invert():
                    dve.wait_ge(s_open, (b + 2) * TB)
                    nc.vector.reciprocal(inv[:, :], sums[:, :, 0]).then_inc(s_step, 1)

                def residual_high():
                    dve.wait_ge(s_step, base + 1)
                    for i in range(TB):
                        ins = nc.vector.scalar_tensor_tensor(
                            out=y[:, i, :], in0=sums[:, i, 1:XA], scalar=inv[:, i:i + 1],
                            in1=mov[:, b * TB + i, HI:LO], op0=ALU.mult, op1=ALU.add)
                    ins.then_inc(s_step, 1)

                def residual_low():
                    dve.wait_ge(s_step, base + 2)
                    nc.vector.tensor_tensor(y[:, :, :], y[:, :, :], mov[:, ds(b * TB, TB), LO:M1],
                                            ALU.add).then_inc(s_step, 1)

                statistics, moments, variance = norm_rows(nc, dve, s_step, base + 3, y, stats, mv, ve)

                def scale_rows():
                    dve.wait_ge(s_pow, b + 1)
                    dve.wait_ge(s_st, b * 16 + 16)
                    for i in range(TB):
                        ins = nc.vector.tensor_scalar(result[:, i, :], y[:, i, :], mv[:, i, 0:1], rstd[:, i:i + 1],
                                                      ALU.subtract, ALU.mult)
                    ins.then_inc(s_step, 1)

                return {1: gather_sums, 2: invert, 3: residual_high, 4: residual_low, 5: statistics, 6: moments,
                        7: variance, 9: scale_rows}

            def block_weights(b, steps):
                for g in range(NG):
                    if g % CG == 0:
                        spread(b, g // CG)
                    make_weights(b, g)
                    if g % CG:
                        make_low(b, g - 1)
                    if g % CG == CG - 1:
                        make_low(b, g)
                    if g in steps:
                        steps[g]()

            block_weights(0, {})
            with dve.Fori(1, NB) as b:
                block_weights(b, finish(b - 1))
            for step in finish(NB - 1).values():
                step()


def kernel(**inputs):
    import concourse.bacc as bacc
    from concourse.bass_utils import run_bass_kernel_spmd

    nc = bacc.Bacc("TRN2", target_bir_lowering=False, num_devices=1)
    row = np.arange(P)
    arrays = {"in_ident": np.eye(P, dtype=np.float32),
              "in_powers": np.where(row[:, None] % WPT == np.arange(WPT)[None, :],
                               2.0 ** (row[:, None] // WPT), 0.0).astype(np.float32)}
    names = ["x", "adj", "L0_gnn_inlayer2", "L0_gnn_W1", "L0_gnn_w2", "L0_gnn_b2", "L0_gnn_w3", "L0_gnn_b3",
             "L1_gnn_beta"]
    for name in names:
        a = np.asarray(inputs[name])
        arrays["in_" + name] = np.ascontiguousarray(a.reshape(1, 1) if a.ndim == 0 else a)

    def dram(name):
        a = arrays[name]
        return nc.dram_tensor(name, a.shape, mybir.dt.from_np(a.dtype), kind="ExternalInput").ap()

    aps = [dram("in_" + name) for name in names]
    out = nc.dram_tensor("out", (N, D), F32, kind="ExternalOutput").ap()
    build_program(nc, *aps, dram("in_ident"), dram("in_powers"), out)
    r = run_bass_kernel_spmd(nc, [arrays], core_ids=[0])
    return r.results[0]["out"]
```

```python
from contextlib import ExitStack

import numpy as np

import concourse.bass as bass
from concourse import mybir

F32 = mybir.dt.float32
BF16 = mybir.dt.bfloat16
F16 = mybir.dt.float16
U16 = mybir.dt.uint16
U8 = mybir.dt.uint8
ALU = mybir.AluOpType
ACT = mybir.ActivationFunctionType
AX_X = mybir.AxisListType.X
ds = bass.ds

P = 128
N = 8192
D = 128
E2 = 256
JT = N // P
BLK = 512
NB = N // BLK
TB = BLK // P
GJ = 2
NG = JT // GJ
GW = GJ * BLK
CJ = 16
NC = JT // CJ
CG = CJ // GJ
BITS = 16
WPT = P // BITS
WB = BLK // BITS
SJ = 4
NS = JT // SJ
OFF = 2 * NS // NC
XA = D + 1
M0 = 4 * XA
M1 = 264
ONE = 7
HI = 8
LO = HI + D
M1N = M1 - ONE
PC = 8
SLOPE = 0.01
EPS = 1e-5
COS_EPS = 1e-7
BIG = 2.0 ** 100
TINY = 2.0 ** -100
XS = 32.0
MR = 4
AHEAD = 4
E0 = 12
E1 = 6
XR = 3 * D


def wait(eng, sem, value):
    if isinstance(value, int) and value <= 0:
        return
    eng.wait_ge(sem, value)


def build_program(nc, x, adj, in2, w1, w2, b2, w3, b3, beta, ident_d, powers_d, out):
    x_rows = x.rearrange("(t p) d -> p t d", p=P)
    in2_rows = in2.rearrange("(t p) e -> p t e", p=P)
    out_rows = out.rearrange("(t p) d -> p t d", p=P)
    adj_rows = adj.rearrange("(b p t) c -> b p t c", p=P, t=TB)
    f1_dram = nc.dram_tensor("f1_scratch", (JT, P), F32, kind="Internal").ap()
    f1_blocks = f1_dram.rearrange("(b t) p -> b (t p)", t=TB)
    xs_dram = nc.dram_tensor("x1_scratch", (N, XR), F32, kind="Internal").ap()
    xs_rows = xs_dram.rearrange("(t p) d -> p t d", p=P)

    with ExitStack() as whole:
        def keep(name, shape, dtype):
            return whole.enter_context(nc.sbuf_tensor(name, shape, dtype))

        bits = keep("bits", [P, NB * JT * WB], U16)
        ident16 = keep("ident16", [P, P], F16)
        ones16 = keep("ones16", [P, P], BF16)
        mhalf = keep("mhalf", [P, TB], F32)
        beta_scale = keep("beta_scale", [P, 1], F32)
        beta_shift = keep("beta_shift", [P, 1], F32)

        x1_flat = keep("x1_flat", [P, TB * XR], F32)
        f = dict(
            x_blk=keep("x_blk", [P, TB, D], F32),
            x1_flat=x1_flat,
            sums=keep("sums0", [P, TB, XA], F32),
            y=keep("y0", [P, TB, D], F32),
            inv=keep("inv0", [P, TB], F32),
            stats=keep("stats0", [P, TB, 6], F32),
            mv=keep("mv0", [P, TB, 2], F32),
            ve=keep("ve0", [P, TB], F32),
            rstd=keep("rstd0", [P, TB], F32),
            n2=keep("n2", [P, TB], F32),
            rnorm=keep("rnorm", [P, TB], F32),
            x1_rows=x1_flat[:, :].rearrange("p (t d) -> p t d", t=TB),
            x1=x1_flat[:, :].rearrange("p (t d) -> p t d", t=TB)[:, :, 0:D],
            x1_out=x1_flat[:, :].bitcast(F16).rearrange("p (t d) -> p t d", t=TB),
            s_open=whole.enter_context(nc.semaphore("s_open0")),
            s_step=whole.enter_context(nc.semaphore("s_step0")),
            s_x=whole.enter_context(nc.semaphore("s_x")),
            s_pow=whole.enter_context(nc.semaphore("s_pow0")),
            s_rn=whole.enter_context(nc.semaphore("s_rn")),
            s_hi=whole.enter_context(nc.semaphore("s_hi0")),
            s_st=whole.enter_context(nc.semaphore("s_st")),
        )

        with ExitStack() as first:
            def sb(name, shape, dtype):
                return first.enter_context(nc.sbuf_tensor(name, shape, dtype))

            t = dict(
                mov=sb("mov0", [P, JT, M0], BF16),
                f2big=sb("f2big", [P, JT], F32),
                alpha=sb("alpha", [P, JT], F32),
                gamma=sb("gamma", [P, JT], F32),
                powers=sb("powers", [P, WPT], BF16),
                stage=sb("stage", [P, 2 * TB * SJ * P], F32),
                words=first.enter_context(nc.psum_tensor("words", [P, 2, 512], F32)),
                s_adj=[first.enter_context(nc.semaphore(name)) for name in ("s_adj_a", "s_adj_b")],
                s_read=first.enter_context(nc.semaphore("s_read")),
                f1_next=sb("f1_next", [P, BLK], F32),
                s_f1row=first.enter_context(nc.semaphore("s_f1row")),
                s_bits=first.enter_context(nc.semaphore("s_bits")),
                tiny_hi=sb("tiny_hi0", [1, 2 * XA], BF16),
                tiny_lo=sb("tiny_lo0", [1, 2 * XA], BF16),
            )
            prepare(nc, adj_rows, bits, x_rows, in2_rows, w1, w2, b2, w3, b3, beta, ident_d, powers_d, f1_dram, f1_blocks,
                    ident16, ones16, mhalf, beta_scale, beta_shift, t, f)
            layer0(nc, adj_rows, x_rows, f1_blocks, bits, ones16, mhalf, xs_rows, t, f)
        layer1(nc, xs_rows, out_rows, bits, ident16, ones16, mhalf, beta_scale, beta_shift, f)


def load_adj(nc, sp, t, adj_rows, b, c):
    s = c % 2
    wait(sp, t["s_read"], b * NS + (c - 1))
    sp.dma_start(t["stage"][:, s * TB * SJ * P:(s + 1) * TB * SJ * P].rearrange("p (t c) -> p t c", t=TB),
                 adj_rows[b + c // NS, :, :, c % NS * SJ * P:(c % NS + 1) * SJ * P]).then_inc(t["s_adj"][s], 16)


def pack_load(nc, pe, t, b, q):
    s, chunk = q % 2, q // (NS // NC) % 2
    stage16 = t["stage"][:, :].bitcast(BF16)
    pe.wait_ge(t["s_adj"][s], (b * (NS // 2) + q // 2 + 1) * 16)
    if q % (NS // NC) == 0:
        wait(pe, t["s_bits"], b * NC + q // (NS // NC) - 1)
    for j in range(SJ):
        for i in range(TB):
            at = 2 * (((s * TB + i) * SJ + j) * P)
            col = ((q % (NS // NC)) * SJ + j) * WB + i * WPT
            mm = nc.tensor.matmul(t["words"][:, chunk, col:col + WPT], stage16[:, at + 1:at + 2 * P:2],
                                  t["powers"][:, :], start=True, stop=True, skip_group_check=True)
    mm.then_inc(t["s_read"], 1)


def take_words(nc, act, t, bits, b, c):
    act.wait_ge(t["s_read"], (b * NC + c + 1) * (NS // NC))
    nc.scalar.activation(
        bits[:, ds((b * NC + c) * CJ * WB, CJ * WB)].rearrange("p (j g t) -> p j g t", t=TB, g=WPT),
        t["words"][:, c % 2, :].rearrange("p (j t g) -> p j g t", t=TB, g=WPT), ACT.Copy).then_inc(t["s_bits"], 1)


def prepare(nc, adj_rows, bits, x_rows, in2_rows, w1, w2, b2, w3, b3, beta, ident_d, powers_d, f1_dram, f1_blocks,
            ident16, ones16, mhalf, beta_scale, beta_shift, t, f):
    mov, f2big, alpha, gamma = t["mov"], t["f2big"], t["alpha"], t["gamma"]
    tiny_hi, tiny_lo = t["tiny_hi"], t["tiny_lo"]
    STEPS = JT // PC
    RING = 4
    ACT_DX = (1, 2, 3, 5, 6)
    FV = 5
    PAIRS = [range(0, 2), range(2, PC - FV)]
    with ExitStack() as ctx:
        def sb(name, shape, dtype):
            return ctx.enter_context(nc.sbuf_tensor(name, shape, dtype))

        def sem(name):
            return ctx.enter_context(nc.semaphore(name))

        ident = sb("ident", [P, P], F32)
        powers32 = sb("powers32", [P, WPT], F32)
        ones32 = sb("ones32", [P, P], F32)
        w1_sb = sb("w1_sb", [P, E2], F32)
        w_col = sb("w_col", [P, 2], F32)
        w_rep = sb("w_rep", [P, 2, P], F32)
        row3 = sb("row3", [1, 3], F32)
        v = f["x_blk"][:, :, :].rearrange("p (w h) d -> p w (h d)", w=2)
        cols3 = sb("cols3", [P, 3], F32)
        space = sb("space", [P, max(RING * PC * E2, 6 * PC * XA)], F32)
        in2_ring = space[:, 0:RING * PC * E2].rearrange("p (s j e) -> p s j e", s=RING, j=PC)
        in2_t = [sb(f"in2_t{n}", [P, len(pair) * E2], F32) for n, pair in enumerate(PAIRS)]
        v_cols = sb("v_cols", [P, 2, 2], F32)
        product = f["y"][:, :, :].rearrange("p (w h) d -> p w (h d)", w=2)
        f_step = sb("f_step", [P, 2, FV], F32)
        f1 = sb("f1", [P, JT], F32)
        f2 = sb("f2", [P, JT], F32)
        small = sb("small", [P, JT], F32)
        row_max = sb("row_max", [P, JT], F32)
        za = sb("za", [P, JT], F32)
        zg = sb("zg", [P, JT], F32)
        mx = sb("mx", [P, 1], F32)
        mx_one = sb("mx_one", [1, 1], F32)
        mx_all = sb("mx_all", [P, 1], F32)
        b_col = sb("b_col", [P, JT], F32)
        d_col = sb("d_col", [P, JT], F32)
        x_early = [sb("x_own", [P, PC * XA], F32)[:, :], f["x1_flat"][:, 0:PC * XA]]
        x_early = [slot.rearrange("p (j d) -> p j d", j=PC) for slot in x_early]
        wx = space[:, 0:4 * PC * XA].rearrange("p (s w j d) -> p s w j d", s=2, w=2, j=PC)
        x_late = space[:, 4 * PC * XA:6 * PC * XA].rearrange("p (s j d) -> p s j d", s=2, j=PC)
        x_ring = x_early + [x_late[:, 0], x_late[:, 1]]
        f1t = sb("f1t", [JT, P], F32)
        tiny32 = sb("tiny32", [1, 2 * XA], F32)
        ps_t = ctx.enter_context(nc.psum_tensor("ps_t", [P, 2, 2 * E2], F32))
        ps_c = ctx.enter_context(nc.psum_tensor("ps_c", [P, 512], F32))
        ps_f = ctx.enter_context(nc.psum_tensor("ps_f", [P, 512], F32))
        ps_m = ctx.enter_context(nc.psum_tensor("ps_m", [P, 512], F32))
        ps_s = ctx.enter_context(nc.psum_tensor("ps_s", [P, 512], F32))

        s_const = sem("s_const")
        s_in2 = [sem(f"s_in2_{s}") for s in range(RING)]
        s_xin = [sem(f"s_xin_{s}") for s in range(RING)]
        s_turn = sem("s_turn0")
        s_tsb = sem("s_tsb")
        s_fpe = sem("s_fpe")
        s_ones = sem("s_ones")
        s_rep = sem("s_rep")
        s_v = sem("s_v")
        s_vsb = sem("s_vsb")
        s_ttr = sem("s_ttr")
        s_f = sem("s_f")
        s_mx = sem("s_mx")
        s_mrow = sem("s_mrow")
        s_chain = sem("s_chain")
        s_exp = sem("s_exp")
        s_f1t = sem("s_f1t")
        s_f1sb = sem("s_f1sb")
        s_f1out = sem("s_f1out")
        s_bx = sem("s_bx")
        s_dx = sem("s_dx")
        s_dx_act = sem("s_dx_act")
        s_hi = sem("s_hi")
        s_lo = sem("s_lo")
        s_cs = sem("s_cs")
        s_end = sem("s_end")
        block = ctx.enter_context(nc.Block())

        def product_sem(k, w):
            if w == 0:
                return s_bx, k + 1
            by_act = sum(n in ACT_DX for n in range(k + 1))
            return (s_dx_act, by_act) if k in ACT_DX else (s_dx, k + 1 - by_act)

        @block.sync
        def _(sp):
            loads = [(w1_sb[:, :], w1), (ident[:, :], ident_d), (powers32[:, :], powers_d),
                     (w_col[:, 0:1], w2.rearrange("(h o) -> h o", o=1)),
                     (w_col[:, 1:2], w3.rearrange("(h o) -> h o", o=1)),
                     (row3[:, 0:1], b2), (row3[:, 1:2], b3),
                     (row3[:, 2:3], beta.rearrange("(a b) -> a b", a=1))]
            for dst, src in loads:
                sp.dma_start(dst, src).then_inc(s_const, 16)
            sp.wait_ge(s_f, 3)
            for c in range(OFF + 2):
                if c == OFF // 2:
                    sp.wait_ge(s_f1sb, 1)
                    sp.dma_start(f1_dram, f1t[:, :]).then_inc(s_f1out, 16)
                    sp.wait_ge(s_f1out, 16)
                    sp.dma_start(t["f1_next"][:, :], f1_blocks[0:1, :].broadcast_to([P, BLK])).then_inc(t["s_f1row"], 16)
                load_adj(nc, sp, t, adj_rows, 0, c)

        @block.tensor
        def _(pe):
            pe.wait_ge(s_ones, 3)
            pe.wait_ge(s_rep, 2)
            pe.wait_ge(s_const, 16 * 8)
            for w in range(2):
                nc.tensor.matmul(ps_t[:, 0, w * E2:(w + 1) * E2], w_rep[:, w, :], w1_sb[:, :], start=True, stop=True)
            for h in range(2):
                nc.tensor.matmul(ps_c[:, 4 + 2 * h:6 + 2 * h], w1_sb[:, h * P:(h + 1) * P], w_col[:, :],
                                 start=True, stop=True, skip_group_check=True)
            nc.tensor.matmul(ps_c[:, 0:3], ones32[0:1, :], row3[:, :], start=True, stop=True,
                             skip_group_check=True).then_inc(s_v, 1)
            pe.wait_ge(s_vsb, 1)

            def use_turned(k, pair):
                pe.wait_ge(s_tsb, 2 * k + pair + 1)
                for i, tile in enumerate(PAIRS[pair]):
                    col = 2 * (k * (PC - FV) + tile)
                    for h in range(2):
                        mm = nc.tensor.matmul(ps_f[:, col:col + 2], in2_t[pair][:, (2 * i + h) * P:(2 * i + h + 1) * P],
                                              v_cols[:, h, :], start=(h == 0), stop=(h == 1), skip_group_check=True)
                mm.then_inc(s_fpe, 1)

            for k in range(STEPS):
                pe.wait_ge(s_in2[k % RING], (k // RING + 1) * 16)
                for pair in range(2):
                    wait(pe, s_tsb, 2 * (k - 1) + pair + 1)
                    for i, tile in enumerate(PAIRS[pair]):
                        for h in range(2):
                            mm = nc.tensor.transpose(
                                ps_t[:, pair, (2 * i + h) * P:(2 * i + h + 1) * P],
                                in2_ring[:, k % RING, FV + tile, h * P:(h + 1) * P], ident[:, :])
                    mm.then_inc(s_turn, 1)
                    if k:
                        use_turned(k - 1, pair)
                if k in (4, 5, 6):
                    pack_load(nc, pe, t, 0, k - 4)
            for pair in range(2):
                use_turned(STEPS - 1, pair)
            pe.wait_ge(s_mx, 1)
            nc.tensor.transpose(ps_m[0:1, 0:P], mx[:, :], ident[:, :]).then_inc(s_mrow, 1)
            pe.wait_ge(s_mx, 2)
            nc.tensor.matmul(ps_m[:, P:P + 1], ones32[0:1, :], mx_one[:, :], start=True, stop=True,
                             skip_group_check=True).then_inc(s_mrow, 1)
            pe.wait_ge(s_chain, 3)
            nc.tensor.transpose(ps_m[0:JT, 2 * P:3 * P], f1[:, :], ident[:, :]).then_inc(s_f1t, 1)
            load = 3
            for k in range(STEPS):
                pe.wait_ge(s_xin[k % RING], (k // RING + 1) * 16)
                for w in range(2):
                    pe.wait_ge(*product_sem(k, w))
                for j in range(PC):
                    mm = nc.tensor.matmul(ps_s[0:1, 0:XA], ones32[:, 0:1], x_ring[k % RING][:, j, :],
                                          start=False, stop=False, skip_group_check=True)
                mm.then_inc(s_cs, 1)
                if load < OFF:
                    pack_load(nc, pe, t, 0, load)
                    load += 1

        @block.gpsimd
        def _(pool):
            nc.gpsimd.memset(mhalf[:, :], -0.5)
            for k in range(STEPS):
                if k >= RING:
                    pool.wait_ge(s_f, k - RING + 3)
                    pool.wait_ge(s_turn, 2 * (k - RING) + 2)
                if k == 0:
                    pool.wait_ge(s_const, 16 * 8)
                pool.dma_start(in2_ring[:, k % RING, :, :], in2_rows[:, k * PC:(k + 1) * PC, :])\
                    .then_inc(s_in2[k % RING], 16)
            for k in range(STEPS):
                if k == 2:
                    pool.wait_ge(s_f, STEPS + 2)
                    pool.wait_ge(s_turn, 2 * STEPS)
                wait(pool, s_cs, k - RING + 1)
                pool.dma_start(x_ring[k % RING][:, :, 0:D], x_rows[:, k * PC:(k + 1) * PC, :]).then_inc(s_xin[k % RING], 16)

        @block.scalar
        def _(act):
            act.wait_ge(s_v, 1)
            nc.scalar.activation(v[:, :, :], ps_t[:, 0, :].rearrange("p (w e) -> p w e", w=2), ACT.Copy)
            nc.scalar.activation(v_cols[:, :, :], ps_c[:, 4:8].rearrange("p (h w) -> p h w", h=2), ACT.Copy)
            nc.scalar.activation(cols3[:, :], ps_c[:, 0:3], ACT.Copy).then_inc(s_vsb, 1)
            for k in range(STEPS):
                for pair in range(2):
                    act.wait_ge(s_turn, 2 * k + pair + 1)
                    wait(act, s_fpe, 2 * (k - 1) + pair + 1)
                    width = len(PAIRS[pair]) * E2
                    nc.scalar.activation(in2_t[pair][:, :], ps_t[:, pair, 0:width], ACT.Copy).then_inc(s_tsb, 1)
            act.wait_ge(s_chain, 1)
            nc.scalar.activation(b_col[:, :], f2[:, :], ACT.Exp)
            nc.scalar.activation(d_col[:, :], f2[:, :], ACT.Exp, scale=SLOPE).then_inc(s_exp, 1)
            act.wait_ge(s_chain, 7)
            nc.scalar.activation(alpha[:, :], za[:, :], ACT.Exp)
            nc.scalar.activation(gamma[:, :], zg[:, :], ACT.Exp).then_inc(s_exp, 1)
            act.wait_ge(s_exp, 1)
            act.wait_ge(s_vsb, 1)
            nc.scalar.activation(beta_scale[:, :], cols3[:, 2:3], ACT.Copy, scale=1.0 / (XS * XS))
            for k in range(STEPS):
                if k == 3:
                    take_words(nc, act, t, bits, 0, 0)
                if k in ACT_DX:
                    act.wait_ge(s_xin[k % RING], (k // RING + 1) * 16)
                    wait(act, s_lo, 2 * (k - 1))
                    for j in range(PC):
                        ins = nc.scalar.activation(wx[:, k % 2, 1, j, :], x_ring[k % RING][:, j, :], ACT.Copy,
                                                   scale=d_col[:, k * PC + j:k * PC + j + 1])
                    ins.then_inc(s_dx_act, 1)
                for w in range(2):
                    act.wait_ge(*product_sem(k, w))
                    nc.scalar.activation(mov[:, ds(k * PC, PC), 2 * w * XA:(2 * w + 1) * XA],
                                         wx[:, k % 2, w, :, :], ACT.Copy).then_inc(s_hi, 1)

        @block.vector
        def _(dve):
            links = [0]

            def chain(instruction):
                links[0] += 1
                instruction.then_inc(s_chain, 1)
                dve.wait_ge(s_chain, links[0])

            nc.vector.memset(ones16[:, :], 1.0)
            for slot in x_early:
                nc.vector.memset(slot[:, :, D:XA], 1.0)
            nc.vector.memset(ps_s[:, :], 0.0).then_inc(s_ones, 1)
            nc.vector.memset(tiny32[:, :], 0.0).then_inc(s_ones, 1)
            nc.vector.memset(ones32[:, :], 1.0).then_inc(s_ones, 1)
            dve.wait_ge(s_ones, 3)
            nc.vector.memset(small[:, 0:1], 0.0).then_inc(s_f, 2)
            dve.wait_ge(s_const, 16 * 8)
            nc.vector.tensor_copy(ident16[:, :], ident[:, :])
            nc.vector.tensor_copy(t["powers"][:, :], powers32[:, :])
            for w in range(2):
                nc.vector.tensor_scalar(w_rep[:, w, :], ones32[:, :], w_col[:, w:w + 1], None, ALU.mult).then_inc(s_rep, 1)
            dve.wait_ge(s_vsb, 1)
            with dve.Fori(0, STEPS // RING) as n:
                for s in range(RING):
                    k = n * RING + s
                    dve.wait_ge(s_in2[s], n * 16 + 16)
                    for j in range(FV):
                        for w in range(2):
                            c = j * 2 + w
                            if c >= 2:
                                dve.wait_ge(s_ttr, k * 2 * FV + c - 1)
                            elif c == 0:
                                dve.wait_ge(s_f, k + 2)
                            nc.vector.tensor_tensor_reduce(
                                product[:, w, :], in2_ring[:, s, j, :], v[:, w, :], 1.0, 0.0, ALU.mult, ALU.add,
                                f_step[:, w, j:j + 1]).then_inc(s_ttr, 1)
                    dve.wait_ge(s_ttr, (k + 1) * 2 * FV)
                    nc.vector.tensor_copy(f1[:, ds(k * PC, FV)], f_step[:, 0, :])
                    nc.vector.tensor_copy(f2[:, ds(k * PC, FV)], f_step[:, 1, :]).then_inc(s_f, 1)
            dve.wait_ge(s_fpe, 2 * STEPS)
            shares = ps_f[:, 0:2 * (PC - FV) * STEPS].rearrange("p (k j w) -> p w k j", w=2, k=STEPS)
            nc.vector.memset(x_late[:, :, :, D:XA], 1.0)
            for w, f in enumerate((f1, f2)):
                nc.vector.tensor_copy(f[:, :].rearrange("p (k j) -> p k j", k=STEPS)[:, :, FV:PC],
                                      shares[:, w, :, :]).then_inc(s_f, 1)
            dve.wait_ge(s_f, STEPS + 4)
            nc.vector.reduce_max(mx[:, :], f2[:, :], AX_X).then_inc(s_mx, 1)
            dve.wait_ge(s_mrow, 1)
            nc.vector.reduce_max(mx_one[:, :], ps_m[0:1, 0:P], AX_X).then_inc(s_mx, 1)
            dve.wait_ge(s_mrow, 2)
            nc.vector.tensor_copy(mx_all[:, :], ps_m[:, P:P + 1]).then_inc(s_mx, 1)
            dve.wait_ge(s_mx, 3)
            chain(nc.vector.tensor_scalar(f2[:, :], f2[:, :], mx_all[:, 0:1], None, ALU.subtract))
            chain(nc.vector.tensor_scalar(f1[:, :], f1[:, :], cols3[:, 0:1], cols3[:, 1:2], ALU.add, ALU.add))
            chain(nc.vector.tensor_scalar(f1[:, :], f1[:, :], mx_all[:, 0:1], None, ALU.add))
            chain(nc.vector.tensor_scalar(small[:, :], f1[:, :], SLOPE, None, ALU.mult))
            chain(nc.vector.tensor_tensor(row_max[:, :], f1[:, :], small[:, :], ALU.max))
            chain(nc.vector.tensor_tensor(za[:, :], f1[:, :], row_max[:, :], ALU.subtract))
            chain(nc.vector.tensor_tensor(zg[:, :], small[:, :], row_max[:, :], ALU.subtract))
            chain(nc.vector.tensor_scalar(f2big[:, :], f2[:, :], BIG, None, ALU.mult))
            chain(nc.vector.tensor_scalar(beta_shift[:, :], cols3[:, 2:3], -1.0, None, ALU.mult))
            chain(nc.vector.tensor_tensor(beta_shift[:, :], beta_shift[:, :], cols3[:, 2:3], ALU.min))
            dve.wait_ge(s_f1t, 1)
            nc.vector.tensor_copy(f1t[:, :], ps_m[0:JT, 2 * P:3 * P]).then_inc(s_f1sb, 1)
            dve.wait_ge(s_exp, 1)
            def products(k):
                dve.wait_ge(s_xin[k % RING], (k // RING + 1) * 16)
                wait(dve, s_lo, 2 * (k - 1))
                for w, factor in enumerate((b_col, d_col)):
                    if w == 1 and k in ACT_DX:
                        continue
                    nc.vector.tensor_tensor(
                        wx[:, k % 2, w, :, :], x_ring[k % RING],
                        factor[:, k * PC:(k + 1) * PC].unsqueeze(2).to_broadcast([P, PC, XA]), ALU.mult)\
                        .then_inc(product_sem(k, w)[0], 1)

            def low_parts(k):
                for w in range(2):
                    dve.wait_ge(s_hi, k * 2 + w + 1)
                    nc.vector.tensor_tensor(
                        mov[:, k * PC:(k + 1) * PC, (2 * w + 1) * XA:(2 * w + 2) * XA], wx[:, k % 2, w, :, :],
                        mov[:, k * PC:(k + 1) * PC, 2 * w * XA:(2 * w + 1) * XA], ALU.subtract).then_inc(s_lo, 1)

            products(0)
            for k in range(1, STEPS):
                products(k)
                low_parts(k - 1)
            low_parts(STEPS - 1)
            dve.wait_ge(s_cs, STEPS)
            chain(nc.vector.tensor_scalar(tiny32[:, XA:2 * XA], ps_s[0:1, 0:XA], TINY, None, ALU.mult))
            chain(nc.vector.tensor_copy(tiny_hi[:, :], tiny32[:, :]))
            nc.vector.tensor_tensor(tiny_lo[:, :], tiny32[:, :], tiny_hi[:, :], ALU.subtract).then_inc(s_end, 1)


def norm_rows(nc, dve, s_step, done, rows, stats, mv, ve):
    def statistics():
        dve.wait_ge(s_step, done)
        for i in range(TB):
            ins = nc.vector.bn_stats(stats[:, i, :], rows[:, i, :])
        ins.then_inc(s_step, 1)

    def moments():
        dve.wait_ge(s_step, done + 1)
        nc.vector.memset(ve[:, :], 0.0)
        for i in range(TB):
            ins = nc.vector.bn_aggr(mv[:, i, :], stats[:, i, :])
        ins.then_inc(s_step, 1)

    def variance():
        dve.wait_ge(s_step, done + 2)
        nc.vector.tensor_scalar(ve[:, :], mv[:, :, 1], EPS, None, ALU.add).then_inc(s_step, 1)

    return statistics, moments, variance


def x1_steps(nc, dve, f, b):
    base = b * E0
    x_blk, sums, y, inv, stats, mv, ve, rstd, n2, rnorm, x1, x1_out = (
        f[name] for name in ("x_blk", "sums", "y", "inv", "stats", "mv", "ve", "rstd", "n2", "rnorm", "x1", "x1_out"))
    s_open, s_step, s_x, s_pow, s_rn, s_hi, s_st = (
        f[name] for name in ("s_open", "s_step", "s_x", "s_pow", "s_rn", "s_hi", "s_st"))

    def invert():
        dve.wait_ge(s_open, (b + 2) * TB)
        nc.vector.reciprocal(inv[:, :], sums[:, :, D]).then_inc(s_step, 1)

    def residual():
        dve.wait_ge(s_step, base + 1)
        dve.wait_ge(s_x, (b + 1) * 16)
        for i in range(TB):
            ins = nc.vector.scalar_tensor_tensor(
                out=y[:, i, :], in0=sums[:, i, 0:D], scalar=inv[:, i:i + 1], in1=x_blk[:, i, :],
                op0=ALU.mult, op1=ALU.add)
        ins.then_inc(s_step, 1)

    statistics, moments, variance = norm_rows(nc, dve, s_step, base + 2, y, stats, mv, ve)

    def scale_rows():
        dve.wait_ge(s_pow, b + 1)
        dve.wait_ge(s_st, b * 16 + 16)
        for i in range(TB):
            ins = nc.vector.tensor_scalar(x1[:, i, :], y[:, i, :], mv[:, i, 0:1], rstd[:, i:i + 1],
                                          ALU.subtract, ALU.mult)
        ins.then_inc(s_step, 1)

    def norm_a():
        nc.vector.tensor_tensor(n2[:, :], rstd[:, :], rstd[:, :], ALU.mult).then_inc(s_step, 1)

    def norm_b():
        dve.wait_ge(s_step, base + 7)
        nc.vector.tensor_tensor(n2[:, :], n2[:, :], mv[:, :, 1], ALU.mult).then_inc(s_step, 1)

    def norm_c():
        dve.wait_ge(s_step, base + 8)
        nc.vector.tensor_scalar(n2[:, :], n2[:, :], float(D), COS_EPS, ALU.mult, ALU.add)\
            .then_inc(s_step, 1)

    def normed_rows():
        dve.wait_ge(s_rn, b + 1)
        for i in range(TB):
            ins = nc.vector.tensor_scalar(y[:, i, :], x1[:, i, :], rnorm[:, i:i + 1], XS,
                                          ALU.mult, ALU.mult)
        ins.then_inc(s_step, 1)

    def x1_low():
        dve.wait_ge(s_hi, b * 2 + 1)
        nc.vector.tensor_tensor(x1_out[:, :, 3 * D:4 * D], x1, x1_out[:, :, 2 * D:3 * D],
                                ALU.subtract).then_inc(s_step, 1)

    def xn_low():
        dve.wait_ge(s_hi, b * 2 + 2)
        nc.vector.tensor_tensor(x1_out[:, :, 5 * D:6 * D], y[:, :, :], x1_out[:, :, 4 * D:5 * D],
                                ALU.subtract).then_inc(s_step, 1)

    return (invert, residual, statistics, moments, variance, scale_rows, norm_a, norm_b, norm_c, normed_rows,
            x1_low, xn_low)


def x1_high(nc, act, f, b):
    act.wait_ge(f["s_step"], b * E0 + 6)
    nc.scalar.activation(f["x1_out"][:, :, 2 * D:3 * D], f["x1"], ACT.Copy).then_inc(f["s_hi"], 1)


def xn_high(nc, act, f, b):
    act.wait_ge(f["s_step"], b * E0 + 10)
    nc.scalar.activation(f["x1_out"][:, :, 4 * D:5 * D], f["y"][:, :, :], ACT.Copy).then_inc(f["s_hi"], 1)


def row_powers(nc, pool, f, mhalf, b):
    pool.wait_ge(f["s_step"], b * E0 + 5)
    nc.gpsimd.tensor_tensor(f["rstd"][:, :], f["ve"][:, :], mhalf[:, :], ALU.pow).then_inc(f["s_pow"], 1)
    pool.wait_ge(f["s_step"], b * E0 + 9)
    nc.gpsimd.tensor_tensor(f["rnorm"][:, :], f["n2"][:, :], mhalf[:, :], ALU.pow).then_inc(f["s_rn"], 1)


def store_x1(nc, sp, f, xs_rows, b):
    sp.wait_ge(f["s_step"], (b + 1) * E0)
    sp.dma_start(xs_rows[:, ds(b * TB, TB), :], f["x1_rows"]).then_inc(f["s_st"], 16)


def chunk_words(bits, b, c):
    return bits[:, ds((b * NC + c) * CJ * WB, CJ * WB)].rearrange("p (j w) -> p j w", w=WB)


def layer0(nc, adj_rows, x_rows, f1_blocks, bits, ones16, mhalf, xs_rows, t, f):
    mov, f2big, alpha, gamma = t["mov"], t["f2big"], t["alpha"], t["gamma"]
    tiny_hi, tiny_lo = t["tiny_hi"], t["tiny_lo"]
    s_bits = t["s_bits"]
    x_blk, sums, inv, s_open, s_step, s_x, s_st = (
        f[name] for name in ("x_blk", "sums", "inv", "s_open", "s_step", "s_x", "s_st"))
    with ExitStack() as ctx:
        def sb(name, shape, dtype):
            return ctx.enter_context(nc.sbuf_tensor(name, shape, dtype))

        def sem(name):
            return ctx.enter_context(nc.semaphore(name))

        mask = sb("mask0", [P, CJ * BLK], U16)
        side = sb("side", [P, 2, GW], BF16)
        upper = sb("upper", [P, MR, GJ, BLK], BF16)
        lower = sb("lower", [P, MR, GJ, BLK], BF16)
        f1_next, s_f1row = t["f1_next"], t["s_f1row"]
        f1_row = sb("f1_row", [P, BLK], F32)
        part = sb("part0", [P, TB, XA], F32)
        acc = ctx.enter_context(nc.psum_tensor("acc0", [P, TB, 512], F32))
        mask16 = mask[:, :].bitcast(BF16)

        s_f1use = sem("s_f1use")
        s_side = sem("s_side")
        s_mask = sem("s_mask")
        s_upper = sem("s_upper")
        s_lower = sem("s_lower")
        s_used = sem("s_used")
        s_tile = sem("s_tile0")
        s_part = sem("s_part")
        block = ctx.enter_context(nc.Block())

        @block.sync
        def _(sp):
            def load_f1(b):
                wait(sp, s_f1use, b)
                sp.dma_start(f1_next[:, :], f1_blocks[ds(b, 1), :].broadcast_to([P, BLK])).then_inc(s_f1row, 16)

            def load_x(b):
                wait(sp, s_step, (b - 1) * E0 + 2)
                sp.dma_start(x_blk[:, :, :], x_rows[:, ds(b * TB, TB), :]).then_inc(s_x, 16)

            for c in range(OFF + 2, OFF + NS):
                load_adj(nc, sp, t, adj_rows, 0, c)
                if c == OFF + NS // 2:
                    load_f1(1)
                    load_x(0)
            with sp.Fori(1, NB - 1) as b:
                for c in range(OFF, OFF + NS):
                    load_adj(nc, sp, t, adj_rows, b, c)
                    if c == OFF + NS // 2:
                        load_f1(b + 1)
                        load_x(b)
                store_x1(nc, sp, f, xs_rows, b - 1)
            for c in range(OFF, NS):
                load_adj(nc, sp, t, adj_rows, NB - 1, c)
            load_x(NB - 1)
            store_x1(nc, sp, f, xs_rows, NB - 2)
            sp.wait_ge(s_st, 16 * NB)
            sp.wait_ge(s_x, 16 * NB)

        @block.tensor
        def _(pe):
            def block_sums(b, packs):
                for g in range(NG):
                    pe.wait_ge(s_lower, b * NG + g + 1)
                    for i in range(TB):
                        if g == 0:
                            pe.wait_ge(s_open, b * TB + i + 1)
                            for n, row in enumerate((tiny_hi, tiny_lo)):
                                nc.tensor.matmul(acc[:, i, 0:2 * XA], ones16[0:1, :], row[:, :],
                                                 start=(n == 0), stop=False, skip_group_check=True)
                        for j in range(GJ):
                            for w, weights in enumerate((upper, lower)):
                                for half in range(2):
                                    at = (2 * w + half) * XA
                                    mm = nc.tensor.matmul(
                                        acc[:, i, w * XA:(w + 1) * XA],
                                        weights[:, g % MR, j, i * P:(i + 1) * P],
                                        mov[:, g * GJ + j, at:at + XA],
                                        start=False, stop=False, skip_group_check=True)
                        if g == NG - 1 and i < TB - 1:
                            mm.then_inc(s_tile, 1)
                    mm.then_inc(s_used, 1)
                    if g % 2 == 1 and g // 2 < packs:
                        pack_load(nc, pe, t, b, OFF + g // 2)

            with pe.Fori(0, NB - 1) as b:
                block_sums(b, NS)
            block_sums(NB - 1, NS - OFF)

        @block.scalar
        def _(act):
            def finish_part(b):
                act.wait_ge(s_open, (b + 1) * TB)
                for i in range(TB):
                    if i < TB - 1:
                        act.wait_ge(s_tile, b * (TB - 1) + i + 1)
                    else:
                        act.wait_ge(s_used, (b + 1) * NG)
                    nc.scalar.activation(part[:, i, :], acc[:, i, XA:2 * XA], ACT.Copy,
                                         scale=gamma[:, ds(b * TB + i, 1)]).then_inc(s_part, 1)

            def block_sides(b, finish, chunks):
                act.wait_ge(s_f1row, (b + 1) * 16)
                wait(act, s_side, b * NG)
                nc.scalar.activation(f1_row[:, :], f1_next[:, :], ACT.Copy).then_inc(s_f1use, 1)
                act.wait_ge(s_f1use, b + 1)
                for g in range(NG):
                    wait(act, s_upper, b * NG + g - 1)
                    for j in range(GJ):
                        jt = g * GJ + j
                        ins = nc.scalar.activation(side[:, g % 2, j * BLK:(j + 1) * BLK], f1_row[:, :], ACT.Relu,
                                                   bias=f2big[:, jt:jt + 1], scale=BIG)
                    ins.then_inc(s_side, 1)
                    if g % CG == CG - 1 and g // CG + 1 < chunks:
                        take_words(nc, act, t, bits, b, g // CG + 1)
                    if finish:
                        if g == 1:
                            finish_part(b - 1)
                        if g == 18:
                            x1_high(nc, act, f, b - 1)
                        if g == 26:
                            xn_high(nc, act, f, b - 1)

            block_sides(0, False, NC + 1)
            with act.Fori(1, NB - 1) as b:
                block_sides(b, True, NC + 1)
            block_sides(NB - 1, True, NC)
            finish_part(NB - 1)

        @block.gpsimd
        def _(pool):
            with pool.Fori(0, NB - 1) as b:
                row_powers(nc, pool, f, mhalf, b)

        @block.vector
        def _(dve):
            def spread(b, c):
                wait(dve, s_lower, b * NG + c * CG)
                dve.wait_ge(s_bits, b * NC + c + 1)
                source = chunk_words(bits, b, c)
                target = mask[:, :].rearrange("p (j k w) -> p j k w", k=BITS, w=WB)
                for k in range(BITS):
                    shift, op = (14 - k, ALU.logical_shift_left) if k < 15 else (1, ALU.logical_shift_right)
                    ins = nc.vector.tensor_scalar(target[:, :, k, :], source, shift, 0x4000, op, ALU.bitwise_and)
                ins.then_inc(s_mask, 1)

            def make_upper(b, g):
                m = (g % CG) * GW
                dve.wait_ge(s_side, b * NG + g + 1)
                if g % CG == 0:
                    dve.wait_ge(s_mask, b * NC + g // CG + 1)
                wait(dve, s_used, b * NG + g + 1 - MR)
                nc.vector.tensor_tensor(upper[:, g % MR, :, :].rearrange("p j i -> p (j i)"), side[:, g % 2, :],
                                        mask16[:, m:m + GW], ALU.min).then_inc(s_upper, 1)

            def make_lower(b, g):
                m = (g % CG) * GW
                dve.wait_ge(s_upper, b * NG + g + 1)
                nc.vector.tensor_tensor(lower[:, g % MR, :, :].rearrange("p j i -> p (j i)"), mask16[:, m:m + GW],
                                        upper[:, g % MR, :, :].rearrange("p j i -> p (j i)"),
                                        ALU.subtract).then_inc(s_lower, 1)

            def gather_sums(b):
                for i in range(TB):
                    dve.wait_ge(s_part, b * TB + i + 1)
                    nc.vector.scalar_tensor_tensor(
                        out=sums[:, i, :], in0=acc[:, i, 0:XA], scalar=alpha[:, ds(b * TB + i, 1)],
                        in1=part[:, i, :], op0=ALU.mult, op1=ALU.add).then_inc(s_open, 1)

            def finish(b):
                at = (2, 5, 10, 11, 12, 14, 18, 19, 20, 22, 23, 27)
                return {1: lambda: gather_sums(b), **dict(zip(at, x1_steps(nc, dve, f, b)))}

            def block_masks(b, steps):
                for g in range(NG):
                    if g % CG == 0:
                        spread(b, g // CG)
                    make_upper(b, g)
                    if g % CG:
                        make_lower(b, g - 1)
                    if g % CG == CG - 1:
                        make_lower(b, g)
                    if g in steps:
                        steps[g]()

            nc.vector.memset(sums[:, :, :], 0.0).then_inc(s_open, TB)
            nc.vector.memset(inv[:, :], 0.0).then_inc(s_st, 16)
            block_masks(0, {})
            with dve.Fori(1, NB) as b:
                block_masks(b, finish(b - 1))
            gather_sums(NB - 1)


def layer1(nc, xs_rows, out_rows, bits, ident16, ones16, mhalf, beta_scale, beta_shift, f):
    TT = 4
    TL = 2 * TT
    LS = 4
    with ExitStack() as ctx:
        def sb(name, shape, dtype):
            return ctx.enter_context(nc.sbuf_tensor(name, shape, dtype))

        def sem(name):
            return ctx.enter_context(nc.semaphore(name))

        mov_flat = sb("mov1", [P, JT * M1], F16)
        xnt = sb("xnt", [P, 2, N], F16)
        mask = sb("mask1", [P, CJ * BLK // 2], U16)
        exps = sb("exps", [P, 2, GW], F32)
        wts = sb("wts", [P, MR * GW], F32)
        low = sb("low", [P, MR, GJ, BLK], BF16)
        tiny32 = sb("tiny32b", [1, M1N], F32)
        tiny_hi = sb("tiny_hi1", [1, M1N], BF16)
        tiny_lo = sb("tiny_lo1", [1, M1N], BF16)
        part = sb("part1", [P, TB, XA], F32)
        sums = sb("sums1", [P, TB, XA], F32)
        inv = sb("inv1", [P, TB], F32)
        y = sb("y1", [P, TB, D], F32)
        x1_blk = sb("x1_blk", [P, TB * D], F32)
        result = sb("result", [P, TB, D], F32)
        stats = sb("stats1", [P, TB, 6], F32)
        mv = sb("mv1", [P, TB, 2], F32)
        ve = sb("ve1", [P, TB], F32)
        rstd = sb("rstd1", [P, TB], F32)
        shift = sb("shift", [P, TB], F32)
        acc = ctx.enter_context(nc.psum_tensor("acc1", [P, TB, 512], F32))
        scores = ctx.enter_context(nc.psum_tensor("scores", [P, 2, GJ, BLK], F32))
        mask8 = mask[:, :].bitcast(U8)
        wts_hi = wts[:, :].bitcast(BF16)
        mov = mov_flat[:, :].rearrange("p (j m) -> p j m", m=M1)
        mov_rows = mov_flat[:, :].bitcast(F32).rearrange("p (j m) -> p j m", m=M1 // 2)
        xn_rows = wts[:, :].rearrange("p (t d) -> p t d", d=D)
        xn_in = wts[:, :].bitcast(F16).rearrange("p (t d) -> p t d", d=2 * D)

        s_mov = [sem(f"s_mov_{k}") for k in range(JT // TL)]
        s_one = sem("s_one")
        s_xn = [sem(f"s_xn_{k}") for k in range(LS)]
        s_turn = sem("s_turn")
        s_thi = sem("s_thi")
        s_tlo = sem("s_tlo")
        s_cs = sem("s_cs1")
        s_tiny = sem("s_tiny")
        s_scores = sem("s_scores")
        s_exps = sem("s_exps")
        s_mask = sem("s_mask1")
        s_wts = sem("s_wts")
        s_low = sem("s_low")
        s_used = sem("s_used1")
        s_tile = sem("s_tile1")
        s_part = sem("s_part1")
        s_open = sem("s_open1")
        s_step = sem("s_step1")
        s_pow = sem("s_pow1")
        s_x = sem("s_x1")
        s_norm = sem("s_norm")
        s_st = sem("s_st1")
        block = ctx.enter_context(nc.Block())

        @block.sync
        def _(sp):
            for k in range(JT // TL):
                if k == JT // TL - 1:
                    sp.wait_ge(f["s_st"], 16 * (NB + 1))
                wait(sp, s_turn, 2 * (k - LS + 1))
                at = k % LS * TL
                sp.dma_start(xn_rows[:, at:at + TL, :], xs_rows[:, k * TL:(k + 1) * TL, 2 * D:3 * D])\
                    .then_inc(s_xn[k % LS], 16)
                sp.dma_start(mov_rows[:, k * TL:(k + 1) * TL, HI // 2:M1 // 2],
                             xs_rows[:, k * TL:(k + 1) * TL, D:2 * D]).then_inc(s_mov[k], 16)
                if k == LS:
                    store_x1(nc, sp, f, xs_rows, NB - 1)

            def load_x1(b):
                wait(sp, s_step, (b - 1) * E1 + 2)
                sp.dma_start(x1_blk[:, :].rearrange("p (t d) -> p t d", t=TB), xs_rows[:, ds(b * TB, TB), 0:D])\
                    .then_inc(s_x, 16)

            def store(b):
                sp.wait_ge(s_norm, (b + 2) * TB)
                sp.dma_start(out_rows[:, ds(b * TB, TB), :], result[:, :, :]).then_inc(s_st, 16)

            load_x1(0)
            with sp.Fori(1, NB) as b:
                load_x1(b)
                store(b - 1)
            store(NB - 1)
            sp.wait_ge(s_st, 16 * (NB + 1))

        @block.tensor
        def _(pe):
            pe.wait_ge(s_one, 1)
            for k in range(JT // TT):
                load = k // 2
                if k % 2 == 0:
                    pe.wait_ge(s_xn[load % LS], (load // LS + 1) * 16)
                wait(pe, s_thi, k - 1)
                wait(pe, s_tlo, k - 1)
                for half in range(2):
                    for i in range(TT):
                        mm = nc.tensor.matmul(scores[:, k % 2, half, i * P:(i + 1) * P],
                                              xn_in[:, load % LS * TL + k % 2 * TT + i, half * D:(half + 1) * D],
                                              ident16[:, :],
                                              start=True, stop=True, skip_group_check=True)
                mm.then_inc(s_turn, 1)
                if k % 2 == 1:
                    pe.wait_ge(s_mov[load], 16)
                    for j in range(load * TL, (load + 1) * TL):
                        mm = nc.tensor.matmul(acc[0:1, 0, 0:M1N], ones16[:, 0:1], mov[:, j, ONE:M1],
                                              start=(j == 0), stop=(j == JT - 1), skip_group_check=True)
            mm.then_inc(s_cs, 1)
            pe.wait_ge(s_thi, JT // TT)
            pe.wait_ge(s_tlo, JT // TT)

            def make_scores(b, g, slot, n):
                wait(pe, s_exps, n - 1)
                for j in range(GJ):
                    for m, (left, right) in enumerate(((0, 0), (0, 1), (1, 0))):
                        mm = nc.tensor.matmul(scores[:, slot, j, :],
                                              xnt[:, left, ds((g * GJ + j) * P, P)],
                                              xnt[:, right, ds(b * BLK, BLK)],
                                              start=(m == 0), stop=(m == 2))
                mm.then_inc(s_scores, 1)

            def weigh(b, g, q, first=False, end=False):
                pe.wait_ge(s_low, b * NG + g + 1)
                for i in range(TB):
                    if first:
                        pe.wait_ge(s_open, b * TB + i + 1)
                        for n, row in enumerate((tiny_hi, tiny_lo)):
                            nc.tensor.matmul(acc[:, i, 0:M1N], ones16[0:1, :], row[:, :],
                                             start=(n == 0), stop=False, skip_group_check=True)
                    for j in range(GJ):
                        at = 2 * (((q % MR) * GJ + j) * BLK + i * P)
                        nc.tensor.matmul(acc[:, i, 0:M1N], wts_hi[:, at + 1:at + 2 * P:2],
                                         mov[:, g * GJ + j, ONE:M1], start=False, stop=False, skip_group_check=True)
                        mm = nc.tensor.matmul(acc[:, i, 0:XA], low[:, q % MR, j, i * P:(i + 1) * P],
                                              mov[:, g * GJ + j, ONE:LO], start=False, stop=False, skip_group_check=True)
                    if end and i < TB - 1:
                        mm.then_inc(s_tile, 1)
                mm.then_inc(s_used, 1)

            def block_sums(b, last):
                def chunk(c, start, end):
                    for q in range(CG):
                        g = c * CG + q
                        weigh(b, g, q, start and q == 0, end and q == CG - 1)
                        if not end or q < CG - AHEAD:
                            make_scores(b, g + AHEAD, (q + AHEAD) % 2, b * NG + g + AHEAD)
                        elif not last:
                            make_scores(b + 1, q - (CG - AHEAD), (q + AHEAD) % 2, b * NG + g + AHEAD)

                chunk(0, True, False)
                with pe.Fori(1, NC - 1) as c:
                    chunk(c, False, False)
                chunk(NC - 1, False, True)

            for g in range(AHEAD):
                make_scores(0, g, g % 2, g)
            pe.wait_ge(s_tiny, 1)
            with pe.Fori(0, NB - 1) as b:
                block_sums(b, False)
            block_sums(NB - 1, True)

        @block.scalar
        def _(act):
            for k in range(JT // TT):
                if k == 2:
                    x1_high(nc, act, f, NB - 1)
                if k == 3:
                    xn_high(nc, act, f, NB - 1)
                act.wait_ge(s_turn, k + 1)
                nc.scalar.activation(xnt[:, 0, k * TT * P:(k + 1) * TT * P], scores[:, k % 2, 0, :],
                                     ACT.Copy).then_inc(s_thi, 1)

            def make_exps(b, g):
                act.wait_ge(s_scores, b * NG + g + 1)
                wait(act, s_wts, b * NG + g - 1)
                nc.scalar.activation(exps[:, g % 2, :], scores[:, g % 2, :, :].rearrange("p j i -> p (j i)"), ACT.Exp,
                                     bias=beta_shift[:, 0:1], scale=beta_scale[:, 0:1]).then_inc(s_exps, 1)

            def finish_part(b):
                act.wait_ge(s_open, (b + 1) * TB)
                for i in range(TB):
                    if i < TB - 1:
                        act.wait_ge(s_tile, b * (TB - 1) + i + 1)
                    else:
                        act.wait_ge(s_used, (b + 1) * NG)
                    nc.scalar.activation(part[:, i, 1:XA], acc[:, i, XA:M1N], ACT.Copy).then_inc(s_part, 1)

            def finish_norm(b):
                act.wait_ge(s_step, (b + 1) * E1)
                act.wait_ge(s_st, b * 16 + 16)
                for i in range(TB):
                    nc.scalar.activation(result[:, i, :], y[:, i, :], ACT.Identity, bias=shift[:, i:i + 1],
                                         scale=rstd[:, i:i + 1]).then_inc(s_norm, 1)

            def block_exps(b, finish):
                for g in range(NG):
                    make_exps(b, g)
                    if finish and g == 1:
                        finish_part(b - 1)
                    if finish and g == 18:
                        finish_norm(b - 1)

            block_exps(0, False)
            with act.Fori(1, NB) as b:
                block_exps(b, True)
            finish_part(NB - 1)
            finish_norm(NB - 1)

        @block.gpsimd
        def _(pool):
            row_powers(nc, pool, f, mhalf, NB - 1)
            with pool.Fori(0, NB) as b:
                pool.wait_ge(s_step, b * E1 + 5)
                nc.gpsimd.tensor_tensor(rstd[:, :], ve[:, :], mhalf[:, :], ALU.pow).then_inc(s_pow, 1)

        @block.vector
        def _(dve):
            nc.vector.memset(mov[:, :, ONE:HI], 1.0).then_inc(s_one, 1)
            nc.vector.memset(part[:, :, 0:1], 0.0).then_inc(s_open, TB)
            nc.vector.memset(inv[:, :], 0.0).then_inc(s_st, 16)
            nc.vector.memset(ve[:, :], 0.0).then_inc(s_norm, TB)
            steps = x1_steps(nc, dve, f, NB - 1)
            before = {0: steps[0:5], 1: steps[5:7], 2: steps[7:9], 3: steps[9:11], 4: steps[11:12]}
            for k in range(JT // TT):
                for step in before.get(k, ()):
                    step()
                dve.wait_ge(s_turn, k + 1)
                nc.vector.tensor_copy(xnt[:, 1, k * TT * P:(k + 1) * TT * P], scores[:, k % 2, 1, :]).then_inc(s_tlo, 1)
            dve.wait_ge(s_cs, 1)
            nc.vector.tensor_scalar(tiny32[:, :], acc[0:1, 0, 0:M1N], TINY, None, ALU.mult).then_inc(s_cs, 1)
            dve.wait_ge(s_cs, 2)
            nc.vector.tensor_copy(tiny_hi[:, :], tiny32[:, :]).then_inc(s_cs, 1)
            dve.wait_ge(s_cs, 3)
            nc.vector.tensor_tensor(tiny_lo[:, :], tiny32[:, :], tiny_hi[:, :], ALU.subtract).then_inc(s_tiny, 1)

            def spread(b, c):
                wait(dve, s_wts, b * NG + c * CG)
                source = chunk_words(bits, b, c)
                target = mask[:, :].rearrange("p (j k w) -> p j k w", k=BITS // 2, w=WB)
                for k in range(BITS // 2):
                    ins = nc.vector.tensor_scalar(target[:, :, k, :], source, k, 0x0101,
                                                  ALU.logical_shift_right, ALU.bitwise_and)
                ins.then_inc(s_mask, 1)

            def make_weights(b, g):
                m = (g % CG) * GW
                at = (g % MR) * GW
                dve.wait_ge(s_exps, b * NG + g + 1)
                if g % CG == 0:
                    dve.wait_ge(s_mask, b * NC + g // CG + 1)
                wait(dve, s_used, b * NG + g + 1 - MR)
                rows = "p (j h r) -> p j h r"
                nc.vector.tensor_tensor(wts[:, at:at + GW].rearrange(rows, j=GJ, h=2),
                                        exps[:, g % 2, :].rearrange(rows, j=GJ, h=2),
                                        mask8[:, m:m + GW].rearrange("p (j r h) -> p j h r", j=GJ, h=2),
                                        ALU.mult).then_inc(s_wts, 1)

            def make_low(b, g):
                at = (g % MR) * GW
                dve.wait_ge(s_wts, b * NG + g + 1)
                nc.vector.tensor_tensor(low[:, g % MR, :, :].rearrange("p j i -> p (j i)"), wts[:, at:at + GW],
                                        wts_hi[:, 2 * at + 1:2 * (at + GW):2], ALU.subtract).then_inc(s_low, 1)

            def finish(b):
                base = b * E1

                def gather_sums():
                    for i in range(TB):
                        dve.wait_ge(s_part, b * TB + i + 1)
                        nc.vector.tensor_tensor(sums[:, i, :], acc[:, i, 0:XA], part[:, i, :], ALU.add)\
                            .then_inc(s_open, 1)

                def invert():
                    dve.wait_ge(s_open, (b + 2) * TB)
                    nc.vector.reciprocal(inv[:, :], sums[:, :, 0]).then_inc(s_step, 1)

                def residual():
                    dve.wait_ge(s_step, base + 1)
                    dve.wait_ge(s_norm, b * TB + TB)
                    dve.wait_ge(s_x, (b + 1) * 16)
                    for i in range(TB):
                        ins = nc.vector.scalar_tensor_tensor(
                            out=y[:, i, :], in0=sums[:, i, 1:XA], scalar=inv[:, i:i + 1],
                            in1=x1_blk[:, i * D:(i + 1) * D], op0=ALU.mult, op1=ALU.add)
                    ins.then_inc(s_step, 1)

                statistics, moments, variance = norm_rows(nc, dve, s_step, base + 2, y, stats, mv, ve)

                def less_mean():
                    dve.wait_ge(s_pow, b + 1)
                    nc.vector.scalar_tensor_tensor(
                        out=shift[:, :], in0=mv[:, :, 0], scalar=-1.0, in1=rstd[:, :],
                        op0=ALU.mult, op1=ALU.mult).then_inc(s_step, 1)

                return {1: gather_sums, 2: invert, 4: residual, 6: statistics, 10: moments, 11: variance,
                        13: less_mean}

            def block_weights(b, steps):
                for g in range(NG):
                    if g % CG == 0:
                        spread(b, g // CG)
                    make_weights(b, g)
                    if g % CG:
                        make_low(b, g - 1)
                    if g % CG == CG - 1:
                        make_low(b, g)
                    if g in steps:
                        steps[g]()

            block_weights(0, {})
            with dve.Fori(1, NB) as b:
                block_weights(b, finish(b - 1))
            for step in finish(NB - 1).values():
                step()


def kernel(**inputs):
    import concourse.bacc as bacc
    from concourse.bass_utils import run_bass_kernel_spmd

    nc = bacc.Bacc("TRN2", target_bir_lowering=False, num_devices=1)
    row = np.arange(P)
    arrays = {"in_ident": np.eye(P, dtype=np.float32),
              "in_powers": np.where(row[:, None] % WPT == np.arange(WPT)[None, :],
                               2.0 ** (row[:, None] // WPT), 0.0).astype(np.float32)}
    names = ["x", "adj", "L0_gnn_inlayer2", "L0_gnn_W1", "L0_gnn_w2", "L0_gnn_b2", "L0_gnn_w3", "L0_gnn_b3",
             "L1_gnn_beta"]
    for name in names:
        a = np.asarray(inputs[name])
        arrays["in_" + name] = np.ascontiguousarray(a.reshape(1, 1) if a.ndim == 0 else a)

    def dram(name):
        a = arrays[name]
        return nc.dram_tensor(name, a.shape, mybir.dt.from_np(a.dtype), kind="ExternalInput").ap()

    aps = [dram("in_" + name) for name in names]
    out = nc.dram_tensor("out", (N, D), F32, kind="ExternalOutput").ap()
    build_program(nc, *aps, dram("in_ident"), dram("in_powers"), out)
    r = run_bass_kernel_spmd(nc, [arrays], core_ids=[0])
    return r.results[0]["out"]
```
